# Optimizing a Trainium2 kernel written in Bass

```python
import numpy as np
import jax
import jax.numpy as jnp

def _softmax(x, axis=-1):
    return jax.nn.softmax(x, axis=axis)

def _gelu(x):
    return jax.nn.gelu(x, approximate=True)

def _silu(x):
    return jax.nn.silu(x)

def _sigmoid(x):
    return jax.nn.sigmoid(x)

def _layernorm(x, axis=-1, eps=1e-05):
    m = jnp.mean(x, axis=axis, keepdims=True)
    v = jnp.var(x, axis=axis, keepdims=True)
    return (x - m) / jnp.sqrt(v + eps)

def _scatter_add(tgt, idx, src, axis=0):
    return tgt.at[idx].add(src)

def _segment_sum(src, seg, n):
    return jax.ops.segment_sum(src, seg, n)
kernel_name = 'mk_seq_postln_d1_jaxref_r8_38e36b'

def setup_inputs(seed: int=0):
    np.random.seed(seed)
    _w = jnp.asarray

    def _L0_attn_setup():
        import jax, jax.numpy as jnp
        import numpy as np
        D_MODEL = 128
        D_STATE = 16
        D_CONV = 4
        EXPAND = 2
        D_INNER = D_MODEL * EXPAND
        BATCH = 4
        SEQ = 256
        DT_MIN = 0.001
        key = jax.random.key(seed)
        ks = jax.random.split(key, 8)
        x = jax.random.normal(ks[0], (BATCH, SEQ, D_MODEL), dtype=jnp.float32)
        in_proj_w = jax.random.normal(ks[1], (2 * D_INNER, D_MODEL), jnp.float32) / np.sqrt(D_MODEL)
        in_proj_b = jnp.zeros((2 * D_INNER,), jnp.float32)
        conv_w = jax.random.normal(ks[2], (D_INNER, 1, D_CONV), jnp.float32) / np.sqrt(D_CONV)
        conv_b = jnp.zeros((D_INNER,), jnp.float32)
        A_log = -jnp.exp(jax.random.normal(ks[3], (D_INNER, D_STATE), jnp.float32) / np.sqrt(D_STATE))
        B_param = jax.random.normal(ks[4], (D_INNER, D_STATE), jnp.float32) / np.sqrt(D_STATE)
        C_param = jax.random.normal(ks[5], (D_INNER, D_STATE), jnp.float32) / np.sqrt(D_STATE)
        log_dt = jnp.full((D_INNER,), np.log(DT_MIN), jnp.float32)
        out_proj_w = jax.random.normal(ks[6], (D_MODEL, D_INNER), jnp.float32) / np.sqrt(D_INNER)
        out_proj_b = jnp.zeros((D_MODEL,), jnp.float32)
        return {'x': x, 'in_proj_w': in_proj_w, 'in_proj_b': in_proj_b, 'conv_w': conv_w, 'conv_b': conv_b, 'A_log': A_log, 'B_param': B_param, 'C_param': C_param, 'log_dt': log_dt, 'out_proj_w': out_proj_w, 'out_proj_b': out_proj_b}
    _L0_attn_in = _L0_attn_setup()

    def _L0_ffn_setup():
        import jax, jax.numpy as jnp
        import numpy as np
        D_MODEL = 128
        EXPERT_DIM = 256
        N_EXPERTS = 8
        LN_EPS = 1e-05

        def _bit_quant(W):
            scale = jnp.clip(jnp.mean(jnp.abs(W), axis=-1, keepdims=True), 1e-05, None)
            w_q = jnp.clip(jnp.round(W / scale), -1.0, 1.0) * scale
            return W + jax.lax.stop_gradient(w_q - W)
        key = jax.random.key(seed)
        ks = jax.random.split(key, 7)
        x = jax.random.normal(ks[0], (4, 256, D_MODEL), dtype=jnp.float32)
        shared_w1 = jax.random.normal(ks[1], (EXPERT_DIM, D_MODEL), dtype=jnp.float32) / np.sqrt(EXPERT_DIM)
        shared_w2 = jax.random.normal(ks[2], (D_MODEL, EXPERT_DIM), dtype=jnp.float32) / np.sqrt(D_MODEL)
        expert_w1 = jax.random.normal(ks[3], (N_EXPERTS, EXPERT_DIM, D_MODEL), dtype=jnp.float32) / np.sqrt(EXPERT_DIM)
        expert_w2 = jax.random.normal(ks[4], (N_EXPERTS, D_MODEL, EXPERT_DIM), dtype=jnp.float32) / np.sqrt(D_MODEL)
        router_w = 0.02 * jax.random.normal(ks[5], (N_EXPERTS, D_MODEL), dtype=jnp.float32)
        ln_gamma = jnp.ones((D_MODEL,), dtype=jnp.float32)
        ln_beta = jnp.zeros((D_MODEL,), dtype=jnp.float32)
        return {'x': x, 'shared_w1': shared_w1, 'shared_w2': shared_w2, 'expert_w1': expert_w1, 'expert_w2': expert_w2, 'router_w': router_w, 'ln_gamma': ln_gamma, 'ln_beta': ln_beta}
    _L0_ffn_in = _L0_ffn_setup()
    _d = {'L0_attn_x': _L0_attn_in['x'], 'L0_attn_in_proj_w': _L0_attn_in['in_proj_w'], 'L0_attn_in_proj_b': _L0_attn_in['in_proj_b'], 'L0_attn_conv_w': _L0_attn_in['conv_w'], 'L0_attn_conv_b': _L0_attn_in['conv_b'], 'L0_attn_A_log': _L0_attn_in['A_log'], 'L0_attn_B_param': _L0_attn_in['B_param'], 'L0_attn_C_param': _L0_attn_in['C_param'], 'L0_attn_log_dt': _L0_attn_in['log_dt'], 'L0_attn_out_proj_w': _L0_attn_in['out_proj_w'], 'L0_attn_out_proj_b': _L0_attn_in['out_proj_b'], 'L0_ffn_shared_w1': _L0_ffn_in['shared_w1'], 'L0_ffn_shared_w2': _L0_ffn_in['shared_w2'], 'L0_ffn_expert_w1': _L0_ffn_in['expert_w1'], 'L0_ffn_expert_w2': _L0_ffn_in['expert_w2'], 'L0_ffn_router_w': _L0_ffn_in['router_w'], 'L0_ffn_ln_gamma': _L0_ffn_in['ln_gamma'], 'L0_ffn_ln_beta': _L0_ffn_in['ln_beta']}
    _x0 = _d['L0_attn_x']
    _d['L0_attn_x'] = jax.random.normal(jax.random.fold_in(jax.random.key(seed), 1), (32, 256, 128), dtype=_x0.dtype)
    del _x0
    return _d

def reference(L0_attn_x, L0_attn_in_proj_w, L0_attn_in_proj_b, L0_attn_conv_w, L0_attn_conv_b, L0_attn_A_log, L0_attn_B_param, L0_attn_C_param, L0_attn_log_dt, L0_attn_out_proj_w, L0_attn_out_proj_b, L0_ffn_shared_w1, L0_ffn_shared_w2, L0_ffn_expert_w1, L0_ffn_expert_w2, L0_ffn_router_w, L0_ffn_ln_gamma, L0_ffn_ln_beta):

    def _L0_attn_ref(x, in_proj_w, in_proj_b, conv_w, conv_b, A_log, B_param, C_param, log_dt, out_proj_w, out_proj_b):
        import jax, jax.numpy as jnp
        import numpy as np
        D_MODEL = 128
        D_STATE = 16
        D_CONV = 4
        EXPAND = 2
        D_INNER = D_MODEL * EXPAND
        BATCH = 4
        SEQ = 256
        DT_MIN = 0.001
        silu = jax.nn.silu
        batch, seq_len, _ = x.shape
        xp = x @ in_proj_w.T + in_proj_b
        x1, x2 = jnp.split(xp, 2, axis=-1)
        u = jnp.transpose(x1, (0, 2, 1))
        u = jax.lax.conv_general_dilated(u, conv_w, window_strides=(1,), padding=[(D_CONV - 1, 0)], dimension_numbers=('NCH', 'OIH', 'NCH'), feature_group_count=D_INNER)
        u = u + conv_b[None, :, None]
        u = silu(jnp.transpose(u, (0, 2, 1)))
        dt = jnp.exp(log_dt)
        A = jnp.exp(A_log)
        dA = jnp.exp(dt[:, None] * A)
        dB = dt[:, None] * B_param

        def step(h, u_t):
            h = dA * h + dB * u_t[..., None]
            y = jnp.einsum('bdn,dn->bd', h, C_param)
            return (h, y)
        h0 = jnp.zeros((batch, D_INNER, D_STATE), x.dtype)
        _, ys = jax.lax.scan(step, h0, jnp.transpose(u, (1, 0, 2)))
        x_ssm = jnp.transpose(ys, (1, 0, 2))
        x_gated = x_ssm * silu(x2)
        return x_gated @ out_proj_w.T + out_proj_b

    def _L0_ffn_ref(x, shared_w1, shared_w2, expert_w1, expert_w2, router_w, ln_gamma, ln_beta):
        import jax, jax.numpy as jnp
        import numpy as np
        D_MODEL = 128
        EXPERT_DIM = 256
        N_EXPERTS = 8
        LN_EPS = 1e-05

        def _bit_quant(W):
            scale = jnp.clip(jnp.mean(jnp.abs(W), axis=-1, keepdims=True), 1e-05, None)
            w_q = jnp.clip(jnp.round(W / scale), -1.0, 1.0) * scale
            return W + jax.lax.stop_gradient(w_q - W)
        mu = jnp.mean(x, axis=-1, keepdims=True)
        var = jnp.mean(jnp.square(x - mu), axis=-1, keepdims=True)
        h = (x - mu) / jnp.sqrt(var + LN_EPS) * ln_gamma + ln_beta
        sw1, sw2 = (_bit_quant(shared_w1), _bit_quant(shared_w2))
        shared_out = jax.nn.silu(jnp.einsum('btd,fd->btf', h, sw1)) @ sw2.T
        probs = jax.nn.softmax(h @ router_w.T, axis=-1)
        top_prob = jnp.max(probs, axis=-1)
        top_idx = jnp.argmax(probs, axis=-1)
        ew1, ew2 = (_bit_quant(expert_w1), _bit_quant(expert_w2))
        h1 = jax.nn.silu(jnp.einsum('btd,efd->ebtf', h, ew1))
        eo = jnp.einsum('ebtf,edf->ebtd', h1, ew2)
        gate = jax.nn.one_hot(top_idx, N_EXPERTS, dtype=h.dtype) * top_prob[..., None]
        routed_out = jnp.einsum('ebtd,bte->btd', eo, gate)
        return shared_out + routed_out
    x = L0_attn_x
    x = _layernorm(x + _L0_attn_ref(x, L0_attn_in_proj_w, L0_attn_in_proj_b, L0_attn_conv_w, L0_attn_conv_b, L0_attn_A_log, L0_attn_B_param, L0_attn_C_param, L0_attn_log_dt, L0_attn_out_proj_w, L0_attn_out_proj_b), axis=-1)
    x = _layernorm(x + _L0_ffn_ref(x, L0_ffn_shared_w1, L0_ffn_shared_w2, L0_ffn_expert_w1, L0_ffn_expert_w2, L0_ffn_router_w, L0_ffn_ln_gamma, L0_ffn_ln_beta), axis=-1)
    return x

_drawn_inputs = setup_inputs


def setup_inputs(seed=0):
    import zlib

    import numpy as np

    out = dict(_drawn_inputs(seed))
    spreads = {'L0_attn_in_proj_b': (0.0, 0.8),
     'L0_attn_conv_b': (0.0, 0.8),
     'L0_attn_log_dt': (-6.907755374908447, 0.6),
     'L0_attn_out_proj_b': (0.0, 0.8),
     'L0_ffn_ln_gamma': (1.0, 0.2),
     'L0_ffn_ln_beta': (0.0, 0.29)}
    factors = {'L0_attn_in_proj_w': 2.963,
     'L0_attn_conv_w': 6.383,
     'L0_attn_A_log': 31.91,
     'L0_attn_C_param': 2.716,
     'L0_attn_out_proj_w': 2.746}
    for name, (base, spread) in spreads.items():
        noise = np.random.default_rng([zlib.crc32(name.encode()), seed]).standard_normal(out[name].shape)
        drawn = base * np.exp(spread * noise) if base else spread * noise
        out[name] = jnp.asarray(drawn.astype(out[name].dtype))
    for name, factor in factors.items():
        out[name] = (out[name] * factor).astype(out[name].dtype)
    return out
```

```python
from contextlib import ExitStack

import concourse.bass as bass
from concourse import mybir

F32 = mybir.dt.float32
I32 = mybir.dt.int32
ALU = mybir.AluOpType
ACT = mybir.ActivationFunctionType
AX = mybir.AxisListType

P = 128
BATCH, SEQ, DM = 32, 256, 128
TOK = BATCH * SEQ
DI = 256
NH = DI // P
NST = 16
L = 32
CH = SEQ // L
NC = BATCH * CH
NI = 32
TAPS = 4
BLK = 512
NBLK = TOK // BLK
BB = BLK // SEQ
CB = BLK // L
TB = BLK // P
NT = TOK // P
NE = 8
FF = 256
FH = FF // P
ROW = DM + 1
SLOT_TILES = NT + NE
PADW = SEQ + TAPS - 1
EPS = 1e-5
FILL = SLOT_TILES // 3


def build(nc, xT, x, in_wT, in_b, conv_w, conv_b, a_log, b_par, c_par, log_dt, out_wT, out_b,
          sw1, sw2, ew1, ew2, routerT, gamma, beta, out):
    sorted_rows = nc.dram_tensor("sorted_rows", (SLOT_TILES * P, ROW), F32).ap()
    routed_out = nc.dram_tensor("routed_out", (TOK + SLOT_TILES * P, DM), F32).ap()
    x_tiles = x.rearrange("(k j p) d -> k p j d", j=TB, p=P)
    out_tiles = out.rearrange("(k j p) d -> k p j d", j=TB, p=P)
    routed_tiles = routed_out[0:TOK, :].rearrange("(k j p) d -> k p j d", j=TB, p=P)

    with ExitStack() as ctx:
        def sb(name, shape, dt=F32):
            return ctx.enter_context(nc.sbuf_tensor(name, shape, dt))

        def sem(name):
            return ctx.enter_context(nc.semaphore(name))

        bank = [ctx.enter_context(nc.psum_tensor(f"bank{n}", [P, 512], F32)) for n in range(8)]

        u_reg = sb("u_reg", [P, NH * NI * NC])
        t_reg = sb("t_reg", [P, NT * ROW])
        e_reg = sb("e_reg", [P, NH * NI * P])
        o_reg = sb("o_reg", [P, NH * NI * P])
        work = sb("work", [P, 6272])

        u_all = u_reg[:, :].rearrange("p (h i c) -> p h i c", h=NH, i=NI)
        toep = t_reg[:, 0:NH * NI * P].rearrange("p (h i m) -> p h i m", h=NH, i=NI)
        enter = e_reg[:, :].rearrange("p (h i m) -> p h i m", h=NH, i=NI)
        leave = o_reg[:, :].rearrange("p (h i m) -> p h i m", h=NH, i=NI)
        z_rows = t_reg[:, :].rearrange("p (t w) -> p t w", w=ROW)
        hT = o_reg[:, :].rearrange("p (k n) -> p k n", n=BLK)
        xn = e_reg[:, :].rearrange("p (t d) -> p t d", d=DM)

        xT_sb = [work[:, 512 * r:512 * r + 512] for r in range(2)]
        x1p = [[work[:, 1024 + 518 * (2 * r + h):1024 + 518 * (2 * r + h + 1)]
                .rearrange("p (b t) -> p b t", b=BB) for h in range(NH)] for r in range(2)]
        acc = [[work[:, 3100 + 512 * (2 * r + h):3100 + 512 * (2 * r + h + 1)] for h in range(NH)]
               for r in range(3)]
        decay_row = [work[:, 1024 + 256 * r:1280 + 256 * r] for r in range(2)]
        states = [work[:, 1536 + 256 * r:1792 + 256 * r] for r in range(2)]
        gate = [[work[:, 1024 + 512 * (2 * r + h):1536 + 512 * (2 * r + h)] for h in range(NH)] for r in range(2)]
        yT = [[work[:, 3072 + 512 * (2 * r + h):3584 + 512 * (2 * r + h)] for h in range(NH)] for r in range(2)]
        x_in = [sb(f"x_in{r}", [P, TB, DM]) for r in range(2)]
        res = [work[:, 5120 + 512 * r:5632 + 512 * r].rearrange("p (j d) -> p j d", j=TB) for r in range(2)]

        w_in = sb("w_in", [P, 2 * DI])
        w_out = sb("w_out", [P, NH, DM])
        w_rt = sb("w_rt", [P, NE])
        small = sb("small", [P, 16 + 64 + 64])
        in_b_sb = small[:, 0:4]
        conv_w_sb = small[:, 4:12].rearrange("p (h k) -> p h k", h=NH)
        conv_b_sb = small[:, 12:14]
        logdt = small[:, 14:16]
        alog = small[:, 16:48].rearrange("p (h n) -> p h n", h=NH)
        bpar = small[:, 48:80].rearrange("p (h n) -> p h n", h=NH)
        cpar = small[:, 80:112].rearrange("p (h n) -> p h n", h=NH)
        gam = small[:, 112:113]
        bet = small[:, 113:114]
        tap_bias = small[:, 114:116]
        outb = sb("outb", [P, DM])
        ident = sb("ident", [P, P])
        decay = sb("decay", [P, NI])
        first_mask = sb("first_mask", [P, BATCH, CH])
        stats = [sb(f"stats{r}", [P, TB, 6]) for r in range(2)]
        mv = [sb(f"mv{r}", [P, TB, 2]) for r in range(2)]
        rs = [sb(f"rs{r}", [P, 6, TB]) for r in range(2)]
        half_neg = sb("half_neg", [P, TB])
        logits = sb("logits", [P, NE, NT])
        top_p = sb("top_p", [P, NT])
        slot = sb("slot", [P, NT], I32)
        tile_expert = sb("tile_expert", [P, SLOT_TILES], I32)

        sc = u_reg
        dt_ = sc[:, 0:2]
        a_ = sc[:, 8:40].rearrange("p (h n) -> p h n", h=NH)
        db = sc[:, 40:72].rearrange("p (h n) -> p h n", h=NH)
        wk = sc[:, 72:104].rearrange("p (h n) -> p h n", h=NH)
        aexp = sc[:, 104:136].rearrange("p (h n) -> p h n", h=NH)
        t_rev = sc[:, 136:168]
        t_fwd = sc[:, 168:200]
        pw_r = sc[:, 256:1280].rearrange("p (h n t) -> p h n t", h=NH, n=NST)
        pw_f = sc[:, 1280:2304].rearrange("p (h n t) -> p h n t", h=NH, n=NST)
        pw = sc[:, 256:2304]
        esrc = sc[:, 2304:3328].rearrange("p (h n t) -> p h n t", h=NH, n=NST)
        ksrc = sc[:, 3328:4352].rearrange("p (h n t) -> p h n t", h=NH, n=NST)
        kpad = sc[:, 4352:4480].rearrange("p (h t) -> p h t", h=NH)
        osrc = sc[:, 4480:6528].rearrange("p (h t s) -> p h t s", h=NH, s=32)
        dsrc = sc[:, 6528:6560]
        ttr = sc[:, 6592:8640].rearrange("p (h t i) -> p h t i", h=NH, i=NI)
        etr = sc[:, 8640:9664].rearrange("p (h n i) -> p h n i", h=NH, i=NI)
        otr = sc[:, 9664:11712].rearrange("p (h t i) -> p h t i", h=NH, i=NI)
        tsrc = sc[:, 11712:13760].rearrange("p (h t s) -> p h t s", h=NH, s=32)

        GW = (1 + NE) * FF
        nat1 = u_reg[:, 0:GW]
        nat2 = u_reg[:, GW:2 * GW]
        w1T = u_reg[:, 2 * GW:3 * GW]
        w2T = u_reg[:, 3 * GW:4 * GW]
        tern = u_reg[:, 4 * GW:6 * GW]
        v0 = 6 * GW
        scale1 = u_reg[:, v0:v0 + 18]
        scale2 = u_reg[:, v0 + 18:v0 + 27]
        hs12 = u_reg[:, v0 + 32:v0 + 59]
        nhs12 = u_reg[:, v0 + 64:v0 + 91]
        s12 = u_reg[:, v0:v0 + 27]
        rt = [work[:, 512 * n:512 * (n + 1)].rearrange("p (e t) -> p e t", e=NE) for n in range(6)]
        rsm = sb("rsm", [P, 640])
        lead_mask = work[:, 3072:3584].rearrange("p (e t) -> p e t", e=NE)
        tri = work[:, 3584:3712]
        ones = work[:, 3712:3840]
        h1 = [[u_reg[:, v0 + 128 + 512 * (2 * r + h):v0 + 640 + 512 * (2 * r + h)] for h in range(FH)] for r in range(2)]
        zt = [sb(f"zt{r}", [P, ROW]) for r in range(4)]
        hb = [work[:, 128 * r:128 * r + 128] for r in range(2)]
        ab = [work[:, 256 + 256 * r:512 + 256 * r] for r in range(2)]
        aT = [work[:, 768 + 256 * r:1024 + 256 * r] for r in range(2)]
        yt = [work[:, 1280 + 128 * r:1408 + 128 * r] for r in range(4)]
        yb = [work[:, 2048 + 512 * r:2560 + 512 * r].rearrange("p (j d) -> p j d", j=TB) for r in range(2)]
        ob = [work[:, 3072 + 512 * r:3584 + 512 * r].rearrange("p (j d) -> p j d", j=TB) for r in range(2)]
        fill = work[:, 2048:2048 + FILL * ROW].rearrange("p (j w) -> p j w", w=ROW)

        S = {n: sem(n) for n in (
            "params_in", "consts", "tb_act", "tb_dve", "tb_zero", "tb_place_act", "tb_place_dve", "tb_place_pool",
            "xT_in0", "xT_in1", "a_mm", "a_evac", "a_conv", "a_silu", "a_tr",
            "b_s", "b_y", "b_h", "b_d0", "b_evac",
            "x_in0s", "x_in1s", "cT_in0", "cT_in1", "c_x2", "c_gate", "c_ytr", "c_mul", "c_xb", "c_out", "c_r",
            "c_st", "c_ag", "c_rs", "c_xn", "c_z", "c_zt", "c_hT", "c_l", "c_lg",
            "r_dve", "r_exp", "r_pe", "r_cst", "fill_in", "unused", "scat",
            "w_in", "w_q", "w_t", "w_c", "s_up", "s_act", "s_dn", "s_add",
            "d_in0", "d_in1", "d_in2", "d_in3", "d_t", "d_h", "d_up", "d_act", "d_t2", "d_at", "d_o", "d_y",
            "d_sc0", "d_sc1", "d_sc2", "d_sc3",
            "e_in0", "e_in1", "e_y", "e_st", "e_ag", "e_rs", "e_n", "e_out0", "e_out1")}
        NPAR = 12
        block = ctx.enter_context(nc.Block())

        @block.sync
        def _(sp):
            for dst, src in ((w_in[:, :], in_wT), (in_b_sb, in_b), (conv_w_sb, conv_w), (conv_b_sb, conv_b),
                             (logdt, log_dt), (alog, a_log), (bpar, b_par), (cpar, c_par),
                             (w_out[:, :, :], out_wT), (w_rt[:, :], routerT), (gam, gamma), (bet, beta)):
                sp.dma_start(dst, src).then_inc(S["params_in"], 16)
            for k in range(NBLK):
                if k >= 2:
                    sp.wait_ge(S["a_mm"], k - 1)
                sp.dma_start(xT_sb[k % 2], xT[:, k * BLK:(k + 1) * BLK]).then_inc(S[f"xT_in{k % 2}"], 16)
            for k in range(NBLK):
                if k < 2:
                    sp.wait_ge(S["a_mm"], NBLK - 1 + k)
                else:
                    sp.wait_ge(S["c_x2"], k - 1)
                    sp.wait_ge(S["c_r"], k - 1)
                sp.dma_start(xT_sb[k % 2], xT[:, k * BLK:(k + 1) * BLK]).then_inc(S[f"cT_in{k % 2}"], 16)
                sp.dma_start(x_in[k % 2][:, :, :], x_tiles[k]).then_inc(S[f"x_in{k % 2}s"], 16)
            sp.wait_ge(S["c_ytr"], NH * NBLK)
            n1 = nat1.rearrange("p (e h d) -> p e h d", h=FH, d=DM)
            n2 = nat2.rearrange("p (e f) -> p e f", f=FF)
            sp.dma_start(n1[:, 0, :, :], sw1.rearrange("(h p) d -> p h d", p=P)).then_inc(S["w_in"], 16)
            for e in range(NE):
                sp.dma_start(n1[:, 1 + e, :, :], ew1[e].rearrange("(h p) d -> p h d", p=P)).then_inc(S["w_in"], 16)
            sp.dma_start(n2[:, 0, :], sw2).then_inc(S["w_in"], 16)
            sp.dma_start(n2[:, 1:, :], ew2.rearrange("e d f -> d e f")).then_inc(S["w_in"], 16)
            sp.wait_ge(S["scat"], 16 * NT)

            def load(j, q, r):
                if not (isinstance(q, int) and q == 0):
                    sp.wait_ge(S[f"d_sc{r}"], 16 * q)
                sp.dma_start(zt[r][:, :], sorted_rows[bass.ds(j * P, P), :]).then_inc(S[f"d_in{r}"], 16)

            for r in range(4):
                load(r, 0, r)
            with sp.Fori(1, SLOT_TILES // 4) as q:
                for r in range(4):
                    load(q * 4 + r, q, r)
            for r in range(4):
                sp.wait_ge(S[f"d_sc{r}"], 16 * (SLOT_TILES // 4))
            for k in range(NBLK + 1):
                if k < NBLK:
                    if k >= 2:
                        sp.wait_ge(S["e_n"], TB * (k - 1))
                    sp.dma_start(yb[k % 2], routed_tiles[k]).then_inc(S[f"e_in{k % 2}"], 16)
                if k >= 1:
                    m = k - 1
                    sp.wait_ge(S["e_n"], TB * (m + 1))
                    sp.dma_start(out_tiles[m], ob[m % 2]).then_inc(S[f"e_out{m % 2}"], 16)
            for r in range(2):
                sp.wait_ge(S[f"e_out{r}"], 16 * (NBLK // 2))

        @block.tensor
        def _(pe):
            mm = nc.tensor.matmul
            pe.wait_ge(S["params_in"], 16 * NPAR)
            for k in range(NBLK):
                pe.wait_ge(S[f"xT_in{k % 2}"], 16 * (k // 2 + 1))
                if k >= 2:
                    pe.wait_ge(S["a_evac"], 4 * (k - 1))
                for h in range(NH):
                    last = mm(bank[2 * (k % 2) + h][:, :], w_in[:, h * P:(h + 1) * P], xT_sb[k % 2],
                              start=True, stop=True)
                last.then_inc(S["a_mm"], 1)

            pe.wait_ge(S["tb_place_act"], 8)
            pe.wait_ge(S["tb_place_dve"], 8)
            pe.wait_ge(S["tb_place_pool"], 8)
            pe.wait_ge(S["a_tr"], NH * NBLK)
            pe.wait_ge(S["a_evac"], 4 * NBLK)

            def chunk_states(i, r, peel):
                if not peel:
                    pe.wait_ge(S["b_h"], i - 1)
                for h in range(NH):
                    last = mm(bank[4 + r][:, 0:NC], enter[:, h, bass.ds(i, 1), :].rearrange("p a m -> p (a m)"),
                              u_all[:, h, bass.ds(i, 1), :].rearrange("p a m -> p (a m)"),
                              start=(h == 0), stop=(h == NH - 1))
                last.then_inc(S["b_s"], 1)

            def outputs(i, r, peel, then):
                if not peel:
                    pe.wait_ge(S["b_evac"], (i - 1) * 2)
                for h in range(NH):
                    mm(bank[2 * r + h][:, 0:NC], toep[:, h, bass.ds(i, 1), :].rearrange("p a m -> p (a m)"),
                       u_all[:, h, bass.ds(i, 1), :].rearrange("p a m -> p (a m)"), start=True, stop=False)
                then()
                pe.wait_ge(S["b_h"], i + 1)
                hv = states[r].rearrange("p (b c) -> p b c", c=CH)
                for h in range(NH):
                    ov = bank[2 * r + h][:, 0:NC].rearrange("p (b c) -> p b c", c=CH)
                    last = mm(ov[:, :, 1:CH], leave[:, h, bass.ds(i, 1), :].rearrange("p a m -> p (a m)"),
                              hv[:, :, 0:CH - 1], start=False, stop=True)
                last.then_inc(S["b_y"], 1)

            chunk_states(0, 0, True)
            outputs(0, 0, True, lambda: chunk_states(1, 1, True))
            outputs(1, 1, True, lambda: chunk_states(2, 0, False))
            for j in range(1, NI // 2 - 1):
                outputs(j * 2, 0, False, lambda: chunk_states(j * 2 + 1, 1, False))
                outputs(j * 2 + 1, 1, False, lambda: chunk_states(j * 2 + 2, 0, False))
            outputs(NI - 2, 0, False, lambda: chunk_states(NI - 1, 1, False))
            outputs(NI - 1, 1, False, lambda: None)

            def x2(k):
                pe.wait_ge(S[f"cT_in{k % 2}"], 16 * (k // 2 + 1))
                if k:
                    pe.wait_ge(S["c_gate"], NH * k)
                else:
                    pe.wait_ge(S["b_evac"], 2 * NI)
                for h in range(NH):
                    last = mm(bank[h][:, :], w_in[:, DI + h * P:DI + (h + 1) * P], xT_sb[k % 2], start=True, stop=True)
                last.then_inc(S["c_x2"], 1)

            def project(k):
                pe.wait_ge(S["c_mul"], NH * (k + 1))
                if k >= 2:
                    pe.wait_ge(S["c_r"], k - 1)
                for j in range(TB):
                    for h in range(NH):
                        last = mm(bank[2 + k % 2][:, j * P:(j + 1) * P], yT[k % 2][h][:, j * P:(j + 1) * P],
                                  w_out[:, h, :], start=(h == 0), stop=(h == NH - 1))
                last.then_inc(S["c_out"], 1)

            def turn_z(k):
                pe.wait_ge(S["c_z"], TB * (k + 1))
                if k >= 2:
                    pe.wait_ge(S["c_hT"], k - 1)
                for j in range(TB):
                    last = nc.tensor.transpose(bank[4 + k % 2][:, j * P:(j + 1) * P], z_rows[:, TB * k + j, 0:DM],
                                               ident[:, :])
                last.then_inc(S["c_zt"], 1)

            def route(k):
                pe.wait_ge(S["c_hT"], k + 1)
                if k:
                    pe.wait_ge(S["c_lg"], k)
                for j in range(TB):
                    last = mm(bank[6][:, NE * j:NE * (j + 1)], hT[:, k, j * P:(j + 1) * P], w_rt[:, :],
                              start=True, stop=True)
                last.then_inc(S["c_l"], 1)

            x2(0)
            for k in range(NBLK + 2):
                if k + 1 < NBLK:
                    x2(k + 1)
                if k < NBLK:
                    project(k)
                if 1 <= k <= NBLK:
                    turn_z(k - 1)
                if k >= 2:
                    route(k - 2)

            pe.wait_ge(S["r_dve"], 9)
            pe.wait_ge(S["r_cst"], 5)
            mm(bank[7][:, :], tri, rt[1].rearrange("p e t -> p (e t)"), start=True, stop=True)
            mm(bank[5][:, :], ones, rt[1].rearrange("p e t -> p (e t)"), start=True, stop=True).then_inc(S["r_pe"], 1)

            tv = tern[:, :]
            for g in range(9):
                pe.wait_ge(S["w_q"], 14)
                if g >= 2:
                    pe.wait_ge(S["w_c"], g - 1)
                for m in range(4):
                    n = 4 * g + m
                    last = nc.tensor.transpose(bank[2 + g % 2][:, m * P:(m + 1) * P], tv[:, n * P:(n + 1) * P], ident[:, :])
                last.then_inc(S["w_t"], 1)

            pe.wait_ge(S["w_c"], 9)

            def up(k):
                if k >= 2:
                    pe.wait_ge(S["s_act"], FH * (k - 1))
                for h in range(FH):
                    last = mm(bank[2 * (k % 2) + h][:, :], w1T[:, h * P:(h + 1) * P], hT[:, k, :], start=True, stop=True)
                last.then_inc(S["s_up"], 1)

            def down(k):
                pe.wait_ge(S["s_act"], FH * (k + 1))
                if k >= 2:
                    pe.wait_ge(S["s_add"], k - 1)
                elif k == 1:
                    pe.wait_ge(S["r_dve"], 13)
                for j in range(TB):
                    for h in range(FH):
                        last = mm(bank[4 + k % 2][:, j * P:(j + 1) * P], h1[k % 2][h][:, j * P:(j + 1) * P],
                                  w2T[:, h * P:(h + 1) * P], start=(h == 0), stop=(h == FH - 1))
                last.then_inc(S["s_dn"], 1)

            up(0)
            for k in range(NBLK):
                if k + 1 < NBLK:
                    up(k + 1)
                down(k)

            pe.wait_ge(S["s_act"], FH * NBLK)
            pe.wait_ge(S["s_add"], NBLK)
            pe.wait_ge(S["r_dve"], R_LAST)

            def known(v):
                return isinstance(v, int)

            def turn(j, q, r):
                pe.wait_ge(S[f"d_in{r}"], (q + 1) * 16)
                if not (known(j) and j < 2):
                    pe.wait_ge(S["d_h"], j - 1)
                nc.tensor.transpose(bank[r % 2][:, 0:P], zt[r][:, 0:DM], ident[:, :]).then_inc(S["d_t"], 1)

            def expert_up(j, r):
                e = pe.value_load(tile_expert[0:1, bass.ds(j, 1)], min_val=0, max_val=NE - 1)
                pe.wait_ge(S["d_h"], j + 1)
                if not (known(j) and j < 2):
                    pe.wait_ge(S["d_act"], j - 1)
                mm(bank[2 + r % 2][:, 0:FF], hb[r % 2], w1T[:, bass.ds(e * FF + FF, FF)],
                   start=True, stop=True).then_inc(S["d_up"], 1)

            def turn_hidden(j, r):
                pe.wait_ge(S["d_act"], j + 1)
                if not (known(j) and j < 2):
                    pe.wait_ge(S["d_at"], j - 1)
                for h in range(FH):
                    last = nc.tensor.transpose(bank[4 + r % 2][:, h * P:(h + 1) * P], ab[r % 2][:, h * P:(h + 1) * P],
                                               ident[:, :])
                last.then_inc(S["d_t2"], 1)

            def expert_down(j, r):
                e = pe.value_load(tile_expert[0:1, bass.ds(j, 1)], min_val=0, max_val=NE - 1)
                pe.wait_ge(S["d_at"], j + 1)
                if not (known(j) and j < 2):
                    pe.wait_ge(S["d_y"], j - 1)
                for h in range(FH):
                    last = mm(bank[6 + r % 2][:, 0:DM], aT[r % 2][:, h * P:(h + 1) * P],
                              w2T[:, bass.ds(e * FF + (FF + h * P), DM)], start=(h == 0), stop=(h == FH - 1))
                last.then_inc(S["d_o"], 1)

            def pe_steps(j0, q, first=False):
                for r in range(4):
                    turn(j0 + r, q, r)
                    if not first or r >= 1:
                        expert_up(j0 + r - 1, (r - 1) % 4)
                    if not first or r >= 2:
                        turn_hidden(j0 + r - 2, (r - 2) % 4)
                    if not first or r >= 3:
                        expert_down(j0 + r - 3, (r - 3) % 4)

            pe_steps(0, 0, first=True)
            with pe.Fori(1, SLOT_TILES // 4) as q:
                pe_steps(q * 4, q)
            n = SLOT_TILES
            expert_up(n - 1, 3)
            turn_hidden(n - 2, 2)
            expert_down(n - 3, 1)
            turn_hidden(n - 1, 3)
            expert_down(n - 2, 2)
            expert_down(n - 1, 3)

        @block.scalar
        def _(act):
            af = nc.scalar.activation
            act.wait_ge(S["params_in"], 16 * NPAR)
            af(dt_, logdt, ACT.Exp).then_inc(S["tb_act"], 1)
            af(aexp, alog, ACT.Exp).then_inc(S["tb_act"], 1)
            act.wait_ge(S["tb_dve"], 6)
            af(pw, pw, ACT.Exp).then_inc(S["tb_act"], 1)
            act.wait_ge(S["tb_zero"], 6)
            act.wait_ge(S["tb_dve"], TB_TR)
            for h in range(NH):
                for q in range(4):
                    rows = slice(32 * q, 32 * q + 32)
                    af(toep[rows, h, :, 32 * q:32 * q + 32],
                       ttr[rows, h, :, :].rearrange("p t i -> p i t")[:, :, ::-1],
                       ACT.Copy).then_inc(S["tb_place_act"], 1)

            def evac(k):
                act.wait_ge(S["a_mm"], k + 1)
                if k >= 2:
                    act.wait_ge(S["a_conv"], 6 * (k - 1))
                if k >= 3:
                    act.wait_ge(S["a_tr"], NH * (k - 2))
                for h in range(NH):
                    ps = bank[2 * (k % 2) + h][:, :]
                    af(x1p[k % 2][h][:, :, TAPS - 1:], ps.rearrange("p (b t) -> p b t", b=BB), ACT.Identity,
                       bias=in_b_sb[:, h:h + 1]).then_inc(S["a_evac"], 1)
                    af(acc[k % 3][h], ps, ACT.Identity, bias=tap_bias[:, h:h + 1],
                       scale=conv_w_sb[:, h, TAPS - 1:TAPS]).then_inc(S["a_evac"], 1)

            act.wait_ge(S["consts"], 8)
            act.wait_ge(S["tb_dve"], 7)
            evac(0)
            for k in range(NBLK):
                if k + 1 < NBLK:
                    evac(k + 1)
                act.wait_ge(S["a_conv"], 6 * (k + 1))
                for h in range(NH):
                    af(acc[k % 3][h], acc[k % 3][h], ACT.Silu).then_inc(S["a_silu"], 1)

            def b_evac(i, r):
                act.wait_ge(S["b_y"], i + 1)
                for h in range(NH):
                    af(u_all[:, h, bass.ds(i, 1), :].rearrange("p a m -> p (a m)"), bank[2 * r + h][:, 0:NC],
                       ACT.Copy).then_inc(S["b_evac"], 1)

            with act.Fori(0, NI // 2) as j:
                b_evac(j * 2, 0)
                b_evac(j * 2 + 1, 1)

            def gates(k):
                act.wait_ge(S["c_x2"], k + 1)
                if k >= 2:
                    act.wait_ge(S["c_mul"], NH * (k - 1))
                elif k == 0:
                    act.wait_ge(S["b_y"], NI)
                    act.wait_ge(S["fill_in"], 16 * (SLOT_TILES // FILL + 1))
                for h in range(NH):
                    af(gate[k % 2][h], bank[h][:, :], ACT.Silu, bias=in_b_sb[:, 2 + h:3 + h]).then_inc(S["c_gate"], 1)

            def norm_T(k):
                act.wait_ge(S["c_zt"], k + 1)
                af(hT[:, k, :], bank[4 + k % 2][:, :], ACT.Identity, bias=bet, scale=gam).then_inc(S["c_hT"], 1)

            gates(0)
            for k in range(NBLK + 1):
                if k + 1 < NBLK:
                    gates(k + 1)
                if k >= 1:
                    norm_T(k - 1)

            act.wait_ge(S["r_dve"], 2)
            af(rt[0], rt[0], ACT.Exp).then_inc(S["r_exp"], 1)

            for g in range(9):
                act.wait_ge(S["w_t"], g + 1)
                both = u_reg[:, 2 * GW:4 * GW]
                af(both[:, 512 * g:512 * (g + 1)], bank[2 + g % 2][:, :], ACT.Copy).then_inc(S["w_c"], 1)

            for k in range(NBLK):
                act.wait_ge(S["s_up"], k + 1)
                if k >= 2:
                    act.wait_ge(S["s_dn"], k - 1)
                for h in range(FH):
                    af(h1[k % 2][h], bank[2 * (k % 2) + h][:, :], ACT.Silu).then_inc(S["s_act"], 1)

            def known(v):
                return isinstance(v, int)

            def d_norm(j, r):
                act.wait_ge(S["d_t"], j + 1)
                if not (known(j) and j < 2):
                    act.wait_ge(S["d_up"], j - 1)
                af(hb[r % 2], bank[r % 2][:, 0:P], ACT.Identity, bias=bet, scale=gam).then_inc(S["d_h"], 1)

            def d_silu(j, r):
                act.wait_ge(S["d_up"], j + 1)
                if not (known(j) and j < 2):
                    act.wait_ge(S["d_t2"], j - 1)
                af(ab[r % 2], bank[2 + r % 2][:, 0:FF], ACT.Silu).then_inc(S["d_act"], 1)

            act.wait_ge(S["r_dve"], R_LAST)
            for r in range(4):
                d_norm(r, r)
                if r:
                    d_silu(r - 1, r - 1)
            with act.Fori(1, SLOT_TILES // 4) as q:
                for r in range(4):
                    d_norm(q * 4 + r, r)
                    d_silu(q * 4 + (r - 1), (r - 1) % 4)
            d_silu(SLOT_TILES - 1, 3)

        @block.vector
        def _(dve):
            v = nc.vector
            n_tb = [0]

            def table(ins):
                ins.then_inc(S["tb_dve"], 1)
                n_tb[0] += 1

            def settled():
                dve.wait_ge(S["tb_dve"], n_tb[0])

            dve.wait_ge(S["params_in"], 16 * NPAR)
            table(v.tensor_tensor(tap_bias, in_b_sb[:, 0:NH], conv_w_sb[:, :, TAPS - 1], ALU.mult))
            dve.wait_ge(S["tb_act"], 2)
            dtb = dt_.rearrange("p (h a) -> p h a", a=1).broadcast_to([P, NH, NST])
            table(v.tensor_tensor(a_, aexp, dtb, ALU.mult))
            table(v.tensor_tensor(db, bpar, dtb, ALU.mult))
            settled()
            table(v.tensor_tensor(wk, db, cpar, ALU.mult))
            dve.wait_ge(S["consts"], 8)

            def wide(ap):
                return ap.rearrange("p h n -> p (h n)").rearrange("p (m a) -> p m a", a=1).broadcast_to([P, NH * NST, L])

            def times(ap):
                return ap.rearrange("p (a t) -> p a t", a=1).broadcast_to([P, NH * NST, L])

            def flat(ap):
                return ap.rearrange("p h n t -> p (h n) t")

            table(v.tensor_tensor(flat(pw_r), wide(a_), times(t_rev), ALU.mult))
            table(v.tensor_tensor(flat(pw_f), wide(a_), times(t_fwd), ALU.mult))
            dve.wait_ge(S["tb_act"], 3)
            table(v.tensor_tensor(tap_bias, tap_bias, conv_b_sb, ALU.add))
            table(v.tensor_tensor(flat(esrc), flat(pw_r), wide(db), ALU.mult))
            table(v.tensor_tensor(flat(ksrc), flat(pw_r), wide(wk), ALU.mult))
            dve.wait_ge(S["tb_zero"], 6)
            for h in range(NH):
                table(v.tensor_tensor(osrc[:, h, :, 16 * h:16 * h + 16], pw_f[:, h, :, :].rearrange("p n t -> p t n"),
                                      cpar[:, h, :].rearrange("p (a n) -> p a n", a=1).broadcast_to([P, L, NST]), ALU.mult))
            table(v.tensor_copy(dsrc.rearrange("p (h n) -> p h n", h=NH), pw_f[:, :, :, L - 1]))
            settled()
            for h in range(NH):
                table(v.tensor_reduce(kpad[:, h, 0:L], ksrc[:, h, :, :].rearrange("p n t -> p t n"), AX.X, ALU.add))
                table(v.transpose(etr[:, h, :, :].rearrange("p n i -> p (n i)"), esrc[:, h, :, :].rearrange("p n t -> p (n t)")))
                table(v.transpose(otr[:, h, :, :].rearrange("p t i -> p (t i)"), osrc[:, h, :, :].rearrange("p t s -> p (t s)")))
            table(v.transpose(decay[:, :], dsrc))
            settled()
            for h in range(NH):
                for t in range(L):
                    table(v.tensor_copy(tsrc[:, h, t, :], kpad[:, h, t:t + L]))
            settled()
            for h in range(NH):
                table(v.transpose(ttr[:, h, :, :].rearrange("p t i -> p (t i)"), tsrc[:, h, :, :].rearrange("p t s -> p (t s)")))
            assert n_tb[0] == TB_TR, n_tb[0]
            settled()
            for h in range(NH):
                for q in range(4):
                    rows = slice(32 * q, 32 * q + 32)
                    v.tensor_copy(enter[rows, h, :, 32 * q + 16 * h:32 * q + 16 * h + 16],
                                  etr[rows, h, :, :].rearrange("p n i -> p i n")).then_inc(S["tb_place_dve"], 1)

            def conv(k):
                dve.wait_ge(S["a_evac"], 4 * (k + 1))
                for n, tap in enumerate((2, 1, 0)):
                    for h in range(NH):
                        if n:
                            dve.wait_ge(S["a_conv"], 6 * k + 2 * (n - 1) + h + 1)
                        av = acc[k % 3][h].rearrange("p (b t) -> p b t", b=BB)
                        v.scalar_tensor_tensor(out=av, in0=x1p[k % 2][h][:, :, tap:tap + SEQ],
                                               scalar=conv_w_sb[:, h, tap:tap + 1], in1=av, op0=ALU.mult,
                                               op1=ALU.add).then_inc(S["a_conv"], 1)

            def spread(k):
                dve.wait_ge(S["a_silu"], NH * (k + 1))
                if k == 0:
                    dve.wait_ge(S["tb_place_dve"], 8)
                    dve.wait_ge(S["tb_place_act"], 8)
                    dve.wait_ge(S["tb_place_pool"], 8)
                for h in range(NH):
                    v.transpose(u_all[:, h, :, CB * k:CB * (k + 1)].rearrange("p i c -> p c i"),
                                acc[k % 3][h].rearrange("p (c t) -> p c t", t=L)).then_inc(S["a_tr"], 1)

            conv(0)
            for k in range(NBLK):
                if k + 1 < NBLK:
                    conv(k + 1)
                spread(k)

            def scan(i, r, peel):
                dve.wait_ge(S["b_s"], i + 1)
                dve.wait_ge(S["b_d0"], i + 1)
                if not peel:
                    dve.wait_ge(S["b_y"], i - 1)
                v.tensor_tensor_scan(states[r], decay_row[r], bank[4 + r][:, 0:NC], 0.0, ALU.mult,
                                     ALU.add).then_inc(S["b_h"], 1)

            scan(0, 0, True)
            scan(1, 1, True)
            with dve.Fori(1, NI // 2) as j:
                scan(j * 2, 0, False)
                scan(j * 2 + 1, 1, False)

            def gather(k):
                if k == 0:
                    dve.wait_ge(S["b_evac"], 2 * NI)
                    dve.wait_ge(S["fill_in"], 16 * (SLOT_TILES // FILL + 1))
                if k >= 2:
                    dve.wait_ge(S["c_out"], k - 1)
                for h in range(NH):
                    v.transpose(yT[k % 2][h].rearrange("p (c t) -> p c t", t=L),
                                u_all[:, h, :, CB * k:CB * (k + 1)].rearrange("p i c -> p c i")).then_inc(S["c_ytr"], 1)

            def residual(k):
                dve.wait_ge(S["c_out"], k + 1)
                dve.wait_ge(S["c_xb"], k + 1)
                if k >= 2:
                    dve.wait_ge(S["c_z"], TB * (k - 1))
                v.tensor_tensor(res[k % 2], bank[2 + k % 2][:, :].rearrange("p (j d) -> p j d", j=TB),
                                x_in[k % 2][:, :, :], ALU.add).then_inc(S["c_r"], 1)
                dve.wait_ge(S["c_r"], k + 1)
                for j in range(TB):
                    v.bn_stats(stats[k % 2][:, j, :], res[k % 2][:, j, :]).then_inc(S["c_st"], 1)
                if k >= 2:
                    dve.wait_ge(S["c_rs"], k - 1)
                for j in range(TB):
                    dve.wait_ge(S["c_st"], TB * k + j + 1)
                    v.bn_aggr(mv[k % 2][:, j, :], stats[k % 2][:, j, :]).then_inc(S["c_ag"], 1)

            def normalise(k):
                dve.wait_ge(S["c_rs"], k + 1)
                for j in range(TB):
                    v.tensor_scalar(xn[:, TB * k + j, :], res[k % 2][:, j, :], mv[k % 2][:, j, 0:1],
                                    rs[k % 2][:, 1, j:j + 1], ALU.subtract, ALU.mult).then_inc(S["c_xn"], 1)
                for j in range(TB):
                    v.tensor_scalar(z_rows[:, TB * k + j, 0:DM], res[k % 2][:, j, :], mv[k % 2][:, j, 0:1],
                                    rs[k % 2][:, 5, j:j + 1], ALU.subtract, ALU.mult).then_inc(S["c_z"], 1)

            def keep_logits(k):
                dve.wait_ge(S["c_l"], k + 1)
                v.tensor_copy(logits[:, :, TB * k:TB * (k + 1)].rearrange("p e j -> p j e"),
                              bank[6][:, 0:TB * NE].rearrange("p (j e) -> p j e", e=NE)).then_inc(S["c_lg"], 1)

            gather(0)
            for k in range(NBLK + 3):
                if k < NBLK:
                    residual(k)
                if k + 1 < NBLK:
                    gather(k + 1)
                if 1 <= k <= NBLK:
                    normalise(k - 1)
                if k >= 3:
                    keep_logits(k - 3)

            n_r = [0]

            def r_step(ins):
                ins.then_inc(S["r_dve"], 1)
                n_r[0] += 1
                dve.wait_ge(S["r_dve"], n_r[0])

            dve.wait_ge(S["c_lg"], NBLK)
            dve.wait_ge(S["r_cst"], 5)
            dve.wait_ge(S["c_out"], NBLK)
            mx = rsm[:, 0:64]
            best = rsm[:, 64:128]
            cnt = rsm[:, 128:136]
            cnt_i = rsm[:, 136:144].bitcast(I32)
            tiles = rsm[:, 144:152]
            upto = rsm[:, 152:160]
            base = rsm[:, 160:168]
            w8 = rsm[:, 168:176]
            one8 = rsm[:, 176:184]
            sumexp = rsm[:, 192:256]
            posf = rsm[:, 256:320]
            jf = rsm[:, 320:320 + SLOT_TILES]
            ef = rsm[:, 400:400 + SLOT_TILES]

            def over_t(ap):
                return ap.rearrange("p (e a) -> p e a", a=1).broadcast_to([P, NE, NT])

            def over_e(ap):
                return ap.rearrange("p (a t) -> p a t", a=1).broadcast_to([P, NE, NT])

            def by_t(ap):
                return ap.rearrange("p e t -> p t e")

            r_step(v.tensor_reduce(mx, by_t(logits[:, :, :]), AX.X, ALU.max))
            r_step(v.tensor_tensor(rt[0], logits[:, :, :], over_e(mx), ALU.subtract))
            r_step(v.tensor_tensor(rt[1], logits[:, :, :], over_e(mx), ALU.is_equal))
            r_step(v.tensor_tensor(rt[1], rt[1], over_t(w8), ALU.mult))
            r_step(v.tensor_reduce(best, by_t(rt[1]), AX.X, ALU.max))
            r_step(v.tensor_copy(rt[2], over_t(w8)))
            dve.wait_ge(S["r_exp"], 1)
            r_step(v.tensor_reduce(sumexp, by_t(rt[0]), AX.X, ALU.add))
            r_step(v.reciprocal(top_p[:, :], sumexp))
            r_step(v.tensor_tensor(rt[1], rt[2], over_e(best), ALU.is_equal))
            dve.wait_ge(S["r_pe"], 1)
            r_step(v.tensor_copy(rt[2], bank[5][:, :].rearrange("p (e t) -> p e t", e=NE)))
            r_step(v.tensor_tensor_scan(rt[3].rearrange("p e t -> p (e t)"), lead_mask.rearrange("p e t -> p (e t)"),
                                        rt[2].rearrange("p e t -> p (e t)"), 0.0, ALU.mult, ALU.add))
            r_step(v.tensor_tensor(rt[4], rt[3], rt[2], ALU.subtract))
            r_step(v.tensor_tensor(rt[4], bank[7][:, :].rearrange("p (e t) -> p e t", e=NE), rt[4], ALU.add))
            r_step(v.tensor_scalar(cnt, rt[3][:, :, NT - 1], float(P - 1), None, ALU.add))
            r_step(v.tensor_copy(cnt_i, cnt))
            r_step(v.tensor_scalar(cnt_i, cnt_i, 7, None, ALU.arith_shift_right))
            r_step(v.tensor_copy(tiles, cnt_i))
            r_step(v.tensor_tensor_scan(upto, one8, tiles, 0.0, ALU.mult, ALU.add))
            r_step(v.tensor_tensor(base, upto, tiles, ALU.subtract))
            r_step(v.tensor_scalar(base, base, float(P), None, ALU.mult))
            r_step(v.tensor_tensor(rt[4], rt[4], over_t(base), ALU.add))
            r_step(v.tensor_tensor(rt[4], rt[4], rt[1], ALU.mult))
            r_step(v.tensor_reduce(posf, by_t(rt[4]), AX.X, ALU.add))
            r_step(v.tensor_copy(slot[:, :], posf))
            ej = work[:, 4096:4096 + SLOT_TILES * NE].rearrange("p (j e) -> p j e", e=NE)
            r_step(v.tensor_tensor(ej, jf.rearrange("p (j a) -> p j a", a=1).broadcast_to([P, SLOT_TILES, NE]),
                                   upto.rearrange("p (a e) -> p a e", a=1).broadcast_to([P, SLOT_TILES, NE]), ALU.is_ge))
            r_step(v.tensor_reduce(ef, ej, AX.X, ALU.add))
            r_step(v.tensor_scalar(ef, ef, float(NE - 1), None, ALU.min))
            r_step(v.tensor_copy(tile_expert[:, :], ef))
            assert n_r[0] == R_LAST, n_r[0]

            n_w = [0]

            def w_step(ins):
                ins.then_inc(S["w_q"], 1)
                n_w[0] += 1
                dve.wait_ge(S["w_q"], n_w[0])

            dve.wait_ge(S["w_in"], 16 * (NE + 3))
            w_step(v.tensor_reduce(scale1, nat1.rearrange("p (r d) -> p r d", d=DM), AX.X, ALU.add, apply_absolute_value=True))
            w_step(v.tensor_reduce(scale2, nat2.rearrange("p (r f) -> p r f", f=FF), AX.X, ALU.add, apply_absolute_value=True))
            w_step(v.tensor_scalar(scale1, scale1, 1.0 / DM, EPS, ALU.mult, ALU.max))
            w_step(v.tensor_scalar(scale2, scale2, 1.0 / FF, EPS, ALU.mult, ALU.max))
            w_step(v.tensor_scalar(hs12, s12, 0.5, None, ALU.mult))
            w_step(v.tensor_scalar(nhs12, s12, -0.5, None, ALU.mult))
            for nat, lo, n, wd, to in ((nat1, 0, 18, DM, 0), (nat2, 18, 9, FF, GW)):
                def per_row(ap):
                    return ap[:, lo:lo + n].rearrange("p (r a) -> p r a", a=1).broadcast_to([P, n, wd])
                nv = nat.rearrange("p (r d) -> p r d", d=wd)
                tv = tern[:, to:to + GW].rearrange("p (r d) -> p r d", d=wd)
                w_step(v.tensor_tensor(tv, nv, per_row(hs12), ALU.is_gt))
                w_step(v.tensor_tensor(nv, nv, per_row(nhs12), ALU.is_lt))
                w_step(v.tensor_tensor(tv, tv, nv, ALU.subtract))
                w_step(v.tensor_tensor(tv, tv, per_row(s12), ALU.mult))

            for k in range(NBLK):
                dve.wait_ge(S["s_dn"], k + 1)
                xv = xn[:, TB * k:TB * (k + 1), :]
                v.tensor_tensor(xv, bank[4 + k % 2][:, :].rearrange("p (j d) -> p j d", j=TB), xv,
                                ALU.add).then_inc(S["s_add"], 1)

            def known(x_):
                return isinstance(x_, int)

            def d_hidden(j, r):
                dve.wait_ge(S["d_t2"], j + 1)
                if not (known(j) and j < 2):
                    dve.wait_ge(S["d_o"], j - 1)
                v.tensor_copy(aT[r % 2], bank[4 + r % 2][:, 0:FF]).then_inc(S["d_at"], 1)

            def d_rows(j, q, r):
                dve.wait_ge(S["d_o"], j + 1)
                if not (known(q) and q == 0):
                    dve.wait_ge(S[f"d_sc{r}"], q * 16)
                v.tensor_copy(yt[r], bank[6 + r % 2][:, 0:DM]).then_inc(S["d_y"], 1)

            def dve_steps(j0, q, last=False):
                for r in range(4):
                    if not last or r < 3:
                        d_hidden(j0 + (r + 1), (r + 1) % 4)
                    d_rows(j0 + r, q, r)

            d_hidden(0, 0)
            dve_steps(0, 0)
            with dve.Fori(1, SLOT_TILES // 4 - 1) as q:
                dve_steps(q * 4, q)
            dve_steps(SLOT_TILES - 4, SLOT_TILES // 4 - 1, last=True)

            dve.wait_ge(S["d_y"], SLOT_TILES)

            def e_sum(k):
                dve.wait_ge(S[f"e_in{k % 2}"], 16 * (k // 2 + 1))
                for j in range(TB):
                    v.scalar_tensor_tensor(out=yb[k % 2][:, j, :], in0=yb[k % 2][:, j, :],
                                           scalar=top_p[:, TB * k + j:TB * k + j + 1], in1=xn[:, TB * k + j, :],
                                           op0=ALU.mult, op1=ALU.add).then_inc(S["e_y"], 1)
                for j in range(TB):
                    dve.wait_ge(S["e_y"], TB * k + j + 1)
                    v.bn_stats(stats[k % 2][:, j, :], yb[k % 2][:, j, :]).then_inc(S["e_st"], 1)
                if k >= 2:
                    dve.wait_ge(S["e_rs"], k - 1)
                    dve.wait_ge(S["e_n"], TB * (k - 1))
                for j in range(TB):
                    dve.wait_ge(S["e_st"], TB * k + j + 1)
                    v.bn_aggr(mv[k % 2][:, j, :], stats[k % 2][:, j, :]).then_inc(S["e_ag"], 1)

            def e_norm(k):
                dve.wait_ge(S["e_rs"], k + 1)
                if k >= 2:
                    dve.wait_ge(S[f"e_out{k % 2}"], 16 * (k // 2))
                for j in range(TB):
                    v.tensor_scalar(ob[k % 2][:, j, :], yb[k % 2][:, j, :], mv[k % 2][:, j, 0:1],
                                    rs[k % 2][:, 1, j:j + 1], ALU.subtract, ALU.mult).then_inc(S["e_n"], 1)

            e_sum(0)
            for k in range(NBLK):
                if k + 1 < NBLK:
                    e_sum(k + 1)
                e_norm(k)

        @block.gpsimd
        def _(pool):
            g = nc.gpsimd
            g.dma_start(outb[:, :], out_b.rearrange("(a d) -> a d", a=1).broadcast_to([P, DM])).then_inc(S["fill_in"], 16)
            g.memset(work[:, 1024:3096], 0.0).then_inc(S["consts"], 1)
            g.iota(t_rev, pattern=[[-1, L]], base=L - 1, channel_multiplier=0,
                   allow_small_or_imprecise_dtypes=True).then_inc(S["consts"], 1)
            g.iota(t_fwd, pattern=[[1, L]], base=1, channel_multiplier=0,
                   allow_small_or_imprecise_dtypes=True).then_inc(S["consts"], 1)
            g.memset(ident[:, :], 0.0).then_inc(S["consts"], 1)
            g.memset(first_mask[:, :, :], 1.0).then_inc(S["consts"], 1)
            g.memset(half_neg[:, :], -0.5).then_inc(S["consts"], 1)
            pool.wait_ge(S["consts"], 6)
            g.memset(first_mask[:, :, 0:1], 0.0).then_inc(S["consts"], 1)
            g.affine_select(out=ident[:, :], in_=ident[:, :], compare_op=ALU.not_equal, fill=1.0, base=0,
                            pattern=[[-1, P]], channel_multiplier=1).then_inc(S["consts"], 1)
            for ap in (kpad, osrc, toep, enter, leave):
                g.memset(ap, 0.0).then_inc(S["tb_zero"], 1)
            g.memset(rsm[:, 176:184], 1.0).then_inc(S["tb_zero"], 1)
            pool.wait_ge(S["tb_zero"], 6)
            pool.wait_ge(S["tb_dve"], TB_TR)
            for h in range(NH):
                for q in range(4):
                    rows = slice(32 * q, 32 * q + 32)
                    g.tensor_copy(leave[rows, h, :, 32 * q:32 * q + 32],
                                  otr[rows, h, :, :].rearrange("p t i -> p i t")).then_inc(S["tb_place_pool"], 1)

            def multipliers(i, r, peel):
                if not peel:
                    pool.wait_ge(S["b_h"], i - 1)
                g.tensor_tensor(decay_row[r], first_mask[:, :, :].rearrange("p b c -> p (b c)"),
                                decay[:, bass.ds(i, 1)].broadcast_to([P, NC]), ALU.mult).then_inc(S["b_d0"], 1)

            pool.wait_ge(S["a_tr"], NH * NBLK)
            pool.wait_ge(S["consts"], 8)
            multipliers(0, 0, True)
            multipliers(1, 1, True)
            with pool.Fori(1, NI // 2) as j:
                multipliers(j * 2, 0, False)
                multipliers(j * 2 + 1, 1, False)

            g.memset(work[:, 2048:2048 + FILL * ROW], 0.0).then_inc(S["unused"], 1)
            sorted_fill = sorted_rows.rearrange("(n j p) w -> n p j w", j=FILL, p=P)
            for n in range(SLOT_TILES // FILL):
                pool.wait_ge(S["unused"], n + 1)
                pool.wait_ge(S["fill_in"], 16 * (n + 1))
                g.iota(fill[:, :, DM:ROW].bitcast(I32).rearrange("p j a -> p (j a)"), pattern=[[P, FILL]],
                       base=TOK + n * FILL * P, channel_multiplier=1).then_inc(S["unused"], 1)
                pool.wait_ge(S["unused"], n + 2)
                g.dma_start(sorted_fill[n], fill).then_inc(S["fill_in"], 16)
            pool.wait_ge(S["fill_in"], 16 * (SLOT_TILES // FILL + 1))

            def multiply(k):
                pool.wait_ge(S["c_gate"], NH * (k + 1))
                pool.wait_ge(S["c_ytr"], NH * (k + 1))
                for h in range(NH):
                    g.tensor_tensor(yT[k % 2][h], yT[k % 2][h], gate[k % 2][h], ALU.mult).then_inc(S["c_mul"], 1)
                pool.wait_ge(S[f"x_in{k % 2}s"], 16 * (k // 2 + 1))
                g.tensor_tensor(x_in[k % 2][:, :, :], x_in[k % 2][:, :, :],
                                outb[:, :].rearrange("p (a d) -> p a d", a=1).broadcast_to([P, TB, DM]),
                                ALU.add).then_inc(S["c_xb"], 1)

            n_p = [0]
            pool_chain = sem("pool_chain")

            def chain(ins):
                ins.then_inc(pool_chain, 1)
                n_p[0] += 1
                pool.wait_ge(pool_chain, n_p[0])

            def rstd(k):
                pool.wait_ge(S["c_ag"], TB * (k + 1))
                if k >= 2:
                    pool.wait_ge(S["c_z"], TB * (k - 1))
                t, var = rs[k % 2], mv[k % 2][:, :, 1]
                chain(g.tensor_scalar(t[:, 0, :], var, EPS, None, ALU.add))
                chain(g.tensor_tensor(t[:, 1, :], t[:, 0, :], half_neg[:, :], ALU.pow))
                chain(g.tensor_tensor(t[:, 2, :], t[:, 1, :], t[:, 1, :], ALU.mult))
                chain(g.tensor_tensor(t[:, 3, :], t[:, 2, :], var, ALU.mult))
                chain(g.tensor_scalar(t[:, 3, :], t[:, 3, :], EPS, None, ALU.add))
                chain(g.tensor_tensor(t[:, 4, :], t[:, 3, :], half_neg[:, :], ALU.pow))
                g.tensor_tensor(t[:, 5, :], t[:, 4, :], t[:, 1, :], ALU.mult).then_inc(S["c_rs"], 1)

            pool.wait_ge(S["tb_place_pool"], 8)
            multiply(0)
            g.iota(z_rows[:, :, DM:ROW].bitcast(I32).rearrange("p t a -> p (t a)"), pattern=[[P, NT]], base=0,
                   channel_multiplier=1).then_inc(S["r_cst"], 1)
            for k in range(NBLK):
                if k + 1 < NBLK:
                    multiply(k + 1)
                rstd(k)

            pool.wait_ge(S["c_z"], TB * NBLK)
            pool.wait_ge(S["c_out"], NBLK)
            g.memset(lead_mask, 1.0).then_inc(S["r_cst"], 1)
            g.memset(work[:, 3584:3840], 1.0).then_inc(S["r_cst"], 1)
            g.iota(rsm[:, 168:176], pattern=[[-1, NE]], base=NE, channel_multiplier=0,
                   allow_small_or_imprecise_dtypes=True)
            g.iota(rsm[:, 320:320 + SLOT_TILES], pattern=[[1, SLOT_TILES]], base=0, channel_multiplier=0,
                   allow_small_or_imprecise_dtypes=True)
            pool.wait_ge(S["r_cst"], 3)
            g.memset(lead_mask[:, :, 0:1], 0.0).then_inc(S["r_cst"], 1)
            g.affine_select(out=tri, in_=tri, compare_op=ALU.is_gt, fill=0.0, base=0,
                            pattern=[[1, P]], channel_multiplier=-1).then_inc(S["r_cst"], 1)
            pool.wait_ge(S["fill_in"], 16 * (SLOT_TILES // FILL + 1))
            pool.wait_ge(S["r_dve"], 24)
            for t in range(NT):
                g.indirect_dma_start(sorted_rows, bass.IndirectOffsetOnAxis(ap=slot[:, t:t + 1], axis=0),
                                     z_rows[:, t, :], None).then_inc(S["scat"], 16)

            def scatter(j, r):
                pool.wait_ge(S["d_y"], j + 1)
                g.indirect_dma_start(routed_out, bass.IndirectOffsetOnAxis(ap=zt[r][:, DM:ROW].bitcast(I32), axis=0),
                                     yt[r], None).then_inc(S[f"d_sc{r}"], 16)

            for j in range(SLOT_TILES):
                scatter(j, j % 4)

            for k in range(NBLK):
                pool.wait_ge(S["e_ag"], TB * (k + 1))
                if k >= 2:
                    pool.wait_ge(S["e_n"], TB * (k - 1))
                t = rs[k % 2]
                chain(g.tensor_scalar(t[:, 0, :], mv[k % 2][:, :, 1], EPS, None, ALU.add))
                g.tensor_tensor(t[:, 1, :], t[:, 0, :], half_neg[:, :], ALU.pow).then_inc(S["e_rs"], 1)


TB_TR = 85
R_LAST = 28


def kernel(**inputs):
    import numpy as np
    import concourse.bacc as bacc
    from concourse.bass_utils import run_bass_kernel_spmd as run

    a = {k: np.asarray(v) for k, v in inputs.items()}
    rows = np.ascontiguousarray(a["L0_attn_x"].reshape(TOK, DM))

    def halves(w):
        return np.ascontiguousarray(np.moveaxis(w.reshape((-1, P) + w.shape[1:]), 0, 1))

    arrays = {
        "xT": np.ascontiguousarray(rows.T), "x": rows,
        "in_wT": np.ascontiguousarray(a["L0_attn_in_proj_w"].T), "in_b": halves(a["L0_attn_in_proj_b"]),
        "conv_w": halves(a["L0_attn_conv_w"].reshape(DI, TAPS)), "conv_b": halves(a["L0_attn_conv_b"]),
        "a_log": halves(a["L0_attn_A_log"]), "b_par": halves(a["L0_attn_B_param"]),
        "c_par": halves(a["L0_attn_C_param"]), "log_dt": halves(a["L0_attn_log_dt"]),
        "out_wT": halves(a["L0_attn_out_proj_w"].T), "out_b": a["L0_attn_out_proj_b"],
        "sw1": a["L0_ffn_shared_w1"], "sw2": a["L0_ffn_shared_w2"], "ew1": a["L0_ffn_expert_w1"],
        "ew2": a["L0_ffn_expert_w2"], "routerT": np.ascontiguousarray(a["L0_ffn_router_w"].T),
        "gamma": a["L0_ffn_ln_gamma"].reshape(DM, 1), "beta": a["L0_ffn_ln_beta"].reshape(DM, 1),
    }
    nc = bacc.Bacc("TRN2", target_bir_lowering=False, num_devices=1)
    args = [nc.dram_tensor(n, v.shape, F32, kind="ExternalInput").ap() for n, v in arrays.items()]
    out = nc.dram_tensor("out", (TOK, DM), F32, kind="ExternalOutput").ap()
    build(nc, *args, out)
    r = run(nc, [arrays], core_ids=[0])
    return r.results[0]["out"].reshape(BATCH, SEQ, DM)
```

```python
from contextlib import ExitStack

import concourse.bass as bass
from concourse import mybir

F32 = mybir.dt.float32
I32 = mybir.dt.int32
ALU = mybir.AluOpType
ACT = mybir.ActivationFunctionType
AX = mybir.AxisListType

P = 128
BATCH, SEQ, DM = 32, 256, 128
TOK = BATCH * SEQ
DI = 256
NH = DI // P
NST = 16
L = 32
CH = SEQ // L
NC = BATCH * CH
NI = 32
TAPS = 4
BLK = 512
NBLK = TOK // BLK
BB = BLK // SEQ
CB = BLK // L
TB = BLK // P
NT = TOK // P
NE = 8
FF = 256
FH = FF // P
ROW = DM + 1
SLOT_TILES = NT + NE
PADW = SEQ + TAPS - 1
EPS = 1e-5
GRP = 8
FILL = SLOT_TILES // 3


def build(nc, xT, x, in_wT, in_b, conv_w, conv_b, a_log, b_par, c_par, log_dt, out_wT, out_b,
          sw1, sw2, ew1, ew2, routerT, gamma, beta, out):
    sorted_rows = nc.dram_tensor("sorted_rows", (SLOT_TILES * P, ROW), F32).ap()
    routed_out = nc.dram_tensor("routed_out", (TOK + SLOT_TILES * P, DM), F32).ap()
    x_tiles = x.rearrange("(k p j) d -> k p j d", j=TB, p=P)
    out_tiles = out.rearrange("(k p j) d -> k p j d", j=TB, p=P)
    routed_tiles = routed_out[0:TOK, :].rearrange("(k p j) d -> k p j d", j=TB, p=P)
    sorted_slots = sorted_rows.rearrange("(p j) w -> p j w", p=P)

    with ExitStack() as ctx:
        def sb(name, shape, dt=F32):
            return ctx.enter_context(nc.sbuf_tensor(name, shape, dt))

        def sem(name):
            return ctx.enter_context(nc.semaphore(name))

        bank = [ctx.enter_context(nc.psum_tensor(f"bank{n}", [P, 512], F32)) for n in range(8)]

        u_reg = sb("u_reg", [P, NH * NI * NC])
        t_reg = sb("t_reg", [P, NT * ROW])
        e_reg = sb("e_reg", [P, NH * NI * P])
        o_reg = sb("o_reg", [P, NH * NI * P])
        work = sb("work", [P, 7168])

        u_all = u_reg[:, :].rearrange("p (h i c) -> p h i c", h=NH, i=NI)
        toep = t_reg[:, 0:NH * NI * P].rearrange("p (h i m) -> p h i m", h=NH, i=NI)
        enter = e_reg[:, :].rearrange("p (h i m) -> p h i m", h=NH, i=NI)
        leave = o_reg[:, :].rearrange("p (h i m) -> p h i m", h=NH, i=NI)
        z_rows = t_reg[:, :].rearrange("p (t w) -> p t w", w=ROW)
        hT = o_reg[:, :].rearrange("p (k n) -> p k n", n=BLK)
        xn = e_reg[:, :].rearrange("p (t d) -> p t d", d=DM)

        xT_sb = [work[:, 512 * r:512 * r + 512] for r in range(2)]
        x1p = [[work[:, 1024 + 518 * (2 * r + h):1024 + 518 * (2 * r + h + 1)]
                .rearrange("p (b t) -> p b t", b=BB) for h in range(NH)] for r in range(2)]
        acc = [[work[:, 3100 + 512 * (2 * r + h):3100 + 512 * (2 * r + h + 1)] for h in range(NH)]
               for r in range(3)]
        decay_row = [work[:, 1024 + 256 * r:1280 + 256 * r] for r in range(2)]
        states = [work[:, 1536 + 256 * r:1792 + 256 * r] for r in range(2)]
        gate = [[work[:, 1024 + 512 * (2 * r + h):1536 + 512 * (2 * r + h)] for h in range(NH)] for r in range(2)]
        yT = [[work[:, 3072 + 512 * (2 * r + h):3584 + 512 * (2 * r + h)] for h in range(NH)] for r in range(3)]
        late = sb("late", [P, 2048])
        x_in = [late[:, 512 * r:512 * r + 512].rearrange("p (j d) -> p j d", j=TB) for r in range(2)]
        res = [work[:, 6144 + 512 * r:6656 + 512 * r].rearrange("p (j d) -> p j d", j=TB) for r in range(2)]

        w_in = sb("w_in", [P, 2 * DI])
        w_out = sb("w_out", [P, NH, DM])
        w_rt = sb("w_rt", [P, NE])
        small = sb("small", [P, 16 + 64 + 64])
        in_b_sb = small[:, 0:4]
        conv_w_sb = small[:, 4:12].rearrange("p (h k) -> p h k", h=NH)
        conv_b_sb = small[:, 12:14]
        logdt = small[:, 14:16]
        alog = small[:, 16:48].rearrange("p (h n) -> p h n", h=NH)
        bpar = small[:, 48:80].rearrange("p (h n) -> p h n", h=NH)
        cpar = small[:, 80:112].rearrange("p (h n) -> p h n", h=NH)
        gam = small[:, 112:113]
        bet = small[:, 113:114]
        tap_bias = small[:, 114:116]
        outb = sb("outb", [P, DM])
        ident = sb("ident", [P, P])
        decay = sb("decay", [P, NI])
        first_mask = sb("first_mask", [P, BATCH, CH])
        stats = [sb(f"stats{r}", [P, TB, 6]) for r in range(2)]
        mv = [sb(f"mv{r}", [P, TB, 2]) for r in range(2)]
        rs = [sb(f"rs{r}", [P, 6, TB]) for r in range(2)]
        half_neg = sb("half_neg", [P, TB])
        logits = sb("logits", [P, NE, NT])
        top_p = sb("top_p", [P, NT])
        slot = sb("slot", [P, NT], I32)
        tile_expert = sb("tile_expert", [P, SLOT_TILES], I32)

        sc = u_reg
        dt_ = sc[:, 0:2]
        a_ = sc[:, 8:40].rearrange("p (h n) -> p h n", h=NH)
        db = sc[:, 40:72].rearrange("p (h n) -> p h n", h=NH)
        wk = sc[:, 72:104].rearrange("p (h n) -> p h n", h=NH)
        aexp = sc[:, 104:136].rearrange("p (h n) -> p h n", h=NH)
        t_rev = sc[:, 136:168]
        t_fwd = sc[:, 168:200]
        pw_r = sc[:, 256:1280].rearrange("p (h n t) -> p h n t", h=NH, n=NST)
        pw_f = sc[:, 1280:2304].rearrange("p (h n t) -> p h n t", h=NH, n=NST)
        pw = sc[:, 256:2304]
        esrc = sc[:, 2304:3328].rearrange("p (h n t) -> p h n t", h=NH, n=NST)
        ksrc = sc[:, 3328:4352].rearrange("p (h n t) -> p h n t", h=NH, n=NST)
        kpad = sc[:, 4352:4480].rearrange("p (h t) -> p h t", h=NH)
        windows = [bass.AP(sc[:, :].tensor, 4352 + 64 * h, [[NH * NI * NC, P], [1, L], [1, L]]) for h in range(NH)]
        osrc = sc[:, 4480:6528].rearrange("p (h t s) -> p h t s", h=NH, s=32)
        dsrc = sc[:, 6528:6560]
        ttr = sc[:, 6592:8640].rearrange("p (h t i) -> p h t i", h=NH, i=NI)
        etr = sc[:, 8640:9664].rearrange("p (h n i) -> p h n i", h=NH, i=NI)
        otr = late[:, :].rearrange("p (h t i) -> p h t i", h=NH, i=NI)

        GW = (1 + NE) * FF
        nat1 = u_reg[:, 0:GW]
        nat2 = u_reg[:, GW:2 * GW]
        w1T = u_reg[:, 2 * GW:3 * GW]
        w2T = u_reg[:, 3 * GW:4 * GW]
        tern = u_reg[:, 4 * GW:6 * GW]
        v0 = 6 * GW
        scale1 = u_reg[:, v0:v0 + 18]
        scale2 = u_reg[:, v0 + 18:v0 + 27]
        hs12 = u_reg[:, v0 + 32:v0 + 59]
        nhs12 = u_reg[:, v0 + 64:v0 + 91]
        s12 = u_reg[:, v0:v0 + 27]
        rt = [work[:, 512 * n:512 * (n + 1)].rearrange("p (e t) -> p e t", e=NE) for n in range(6)]
        rsm = work[:, 4736:5376]
        lead_mask = work[:, 3072:3584].rearrange("p (e t) -> p e t", e=NE)
        tri = work[:, 3584:3712]
        ones = work[:, 3712:3840]
        h1 = [[u_reg[:, v0 + 128 + 512 * (2 * r + h):v0 + 640 + 512 * (2 * r + h)] for h in range(FH)] for r in range(2)]
        zt = [z_rows[:, m, :] for m in range(GRP)]
        ids = sb("ids", [P, GRP], I32)
        hb = [work[:, 128 * r:128 * r + 128] for r in range(4)]
        w1s = [work[:, 512 + 256 * r:768 + 256 * r] for r in range(4)]
        ab = [work[:, 1536 + 256 * r:1792 + 256 * r] for r in range(4)]
        yt = [work[:, 2560 + 128 * r:2688 + 128 * r] for r in range(GRP)]
        yb = [work[:, 3584 + 512 * r:4096 + 512 * r].rearrange("p (j d) -> p j d", j=TB) for r in range(4)]
        ob = [work[:, 5632 + 512 * r:6144 + 512 * r].rearrange("p (j d) -> p j d", j=TB) for r in range(3)]
        fill = work[:, 2048:2048 + FILL * ROW].rearrange("p (j w) -> p j w", w=ROW)

        S = {n: sem(n) for n in (
            "params_in", "consts", "tb_act", "tb_dve", "tb_zero", "tb_zero_dve", "tb_place_act", "tb_place_dve", "tb_place_pool",
            "xT_in0", "xT_in1", "a_mm", "a_evac", "a_conv", "a_silu", "a_tr",
            "b_s", "b_y", "b_h", "b_d0", "b_evac",
            "x_in0s", "x_in1s", "cT_in0", "cT_in1", "c_x2", "c_gate", "c_ytr", "c_mul", "c_xb", "c_out", "c_r",
            "c_st", "c_ag", "c_rs", "c_xn", "c_z", "c_zt", "c_hT", "c_l", "c_lg",
            "r_dve", "r_exp", "r_pe", "r_cst", "fill_in", "unused", "scat",
            "w_in", "w_q", "w_t", "w_c", "s_up", "s_act", "s_dn", "s_add",
            "d_in0", "d_in1", "d_t", "d_h", "d_w", "d_id", "d_up", "d_act", "d_o", "d_y",
            *(f"d_sc{m}" for m in range(8)), "e_in0", "e_in1", "e_in2", "e_in3", "e_y", "e_st", "e_ag", "e_rs", "e_n",
            "e_out0", "e_out1", "e_out2")}
        NPAR = 12
        block = ctx.enter_context(nc.Block())

        @block.sync
        def _(sp):
            for dst, src in ((w_in[:, :], in_wT), (in_b_sb, in_b), (conv_w_sb, conv_w), (conv_b_sb, conv_b),
                             (logdt, log_dt), (alog, a_log), (bpar, b_par), (cpar, c_par),
                             (w_out[:, :, :], out_wT), (w_rt[:, :], routerT), (gam, gamma), (bet, beta)):
                sp.dma_start(dst, src).then_inc(S["params_in"], 16)
            for k in range(NBLK):
                if k >= 2:
                    sp.wait_ge(S["a_mm"], k - 1)
                sp.dma_start(xT_sb[k % 2], xT[:, k * BLK:(k + 1) * BLK]).then_inc(S[f"xT_in{k % 2}"], 16)
            for k in range(NBLK):
                if k < 2:
                    sp.wait_ge(S["a_mm"], NBLK - 1 + k)
                    sp.wait_ge(S["tb_place_pool"], 8)
                else:
                    sp.wait_ge(S["c_x2"], k - 1)
                    sp.wait_ge(S["c_r"], k - 1)
                sp.dma_start(xT_sb[k % 2], xT[:, k * BLK:(k + 1) * BLK]).then_inc(S[f"cT_in{k % 2}"], 16)
                sp.dma_start(x_in[k % 2], x_tiles[k]).then_inc(S[f"x_in{k % 2}s"], 16)
            sp.wait_ge(S["c_ytr"], NH * NBLK)
            n1 = nat1.rearrange("p (e h d) -> p e h d", h=FH, d=DM)
            n2 = nat2.rearrange("p (e f) -> p e f", f=FF)
            sp.dma_start(n1[:, 0, :, :], sw1.rearrange("(h p) d -> p h d", p=P)).then_inc(S["w_in"], 16)
            for e in range(NE):
                sp.dma_start(n1[:, 1 + e, :, :], ew1[e].rearrange("(h p) d -> p h d", p=P)).then_inc(S["w_in"], 16)
            sp.dma_start(n2[:, 0, :], sw2).then_inc(S["w_in"], 16)
            sp.dma_start(n2[:, 1:, :], ew2.rearrange("e d f -> d e f")).then_inc(S["w_in"], 16)
            sp.wait_ge(S["scat"], 16 * NT)

            def load(q, half):
                if not (isinstance(q, int) and q == 0):
                    sp.wait_ge(S["d_t"], q * GRP - 4 + 4 * half)
                    sp.wait_ge(S["d_id"], q * 2 - 1 + half)
                sp.dma_start(z_rows[:, 4 * half:4 * half + 4, :],
                             sorted_slots[:, bass.ds(q * GRP + 4 * half, 4), :]).then_inc(S[f"d_in{half}"], 16)

            load(0, 0)
            load(0, 1)
            with sp.Fori(1, SLOT_TILES // GRP) as q:
                load(q, 0)
                load(q, 1)
            for m in range(GRP):
                sp.wait_ge(S[f"d_sc{m}"], 16 * (SLOT_TILES // GRP))
            for k in range(NBLK + 3):
                if k < NBLK:
                    if k >= 4:
                        sp.wait_ge(S["e_n"], TB * (k - 3))
                    sp.dma_start(yb[k % 4], routed_tiles[k]).then_inc(S[f"e_in{k % 4}"], 16)
                if k >= 3:
                    m = k - 3
                    sp.wait_ge(S["e_n"], TB * (m + 1))
                    sp.dma_start(out_tiles[m], ob[m % 3]).then_inc(S[f"e_out{m % 3}"], 16)
            for r in range(3):
                sp.wait_ge(S[f"e_out{r}"], 16 * ((NBLK + 2 - r) // 3))

        @block.tensor
        def _(pe):
            mm = nc.tensor.matmul
            pe.wait_ge(S["params_in"], 16 * NPAR)
            for k in range(NBLK):
                pe.wait_ge(S[f"xT_in{k % 2}"], 16 * (k // 2 + 1))
                if k >= 2:
                    pe.wait_ge(S["a_evac"], 4 * (k - 1))
                for h in range(NH):
                    last = mm(bank[2 * (k % 2) + h][:, :], w_in[:, h * P:(h + 1) * P], xT_sb[k % 2],
                              start=True, stop=True)
                last.then_inc(S["a_mm"], 1)

            pe.wait_ge(S["tb_place_act"], 8)
            pe.wait_ge(S["tb_place_dve"], 8)
            pe.wait_ge(S["tb_place_pool"], 8)
            pe.wait_ge(S["a_tr"], NH * NBLK)
            pe.wait_ge(S["a_evac"], 4 * NBLK)

            def chunk_states(i, r, peel):
                if not peel:
                    pe.wait_ge(S["b_h"], i - 1)
                for h in range(NH):
                    last = mm(bank[4 + r][:, 0:NC], enter[:, h, bass.ds(i, 1), :].rearrange("p a m -> p (a m)"),
                              u_all[:, h, bass.ds(i, 1), :].rearrange("p a m -> p (a m)"),
                              start=(h == 0), stop=(h == NH - 1))
                last.then_inc(S["b_s"], 1)

            def outputs(i, r, peel, then):
                if not peel:
                    pe.wait_ge(S["b_evac"], (i - 1) * 2)
                for h in range(NH):
                    mm(bank[2 * r + h][:, 0:NC], toep[:, h, bass.ds(i, 1), :].rearrange("p a m -> p (a m)"),
                       u_all[:, h, bass.ds(i, 1), :].rearrange("p a m -> p (a m)"), start=True, stop=False)
                then()
                pe.wait_ge(S["b_h"], i + 1)
                hv = states[r].rearrange("p (b c) -> p b c", c=CH)
                for h in range(NH):
                    ov = bank[2 * r + h][:, 0:NC].rearrange("p (b c) -> p b c", c=CH)
                    last = mm(ov[:, :, 1:CH], leave[:, h, bass.ds(i, 1), :].rearrange("p a m -> p (a m)"),
                              hv[:, :, 0:CH - 1], start=False, stop=True)
                last.then_inc(S["b_y"], 1)

            chunk_states(0, 0, True)
            outputs(0, 0, True, lambda: chunk_states(1, 1, True))
            outputs(1, 1, True, lambda: chunk_states(2, 0, False))
            for j in range(1, NI // 2 - 1):
                outputs(j * 2, 0, False, lambda: chunk_states(j * 2 + 1, 1, False))
                outputs(j * 2 + 1, 1, False, lambda: chunk_states(j * 2 + 2, 0, False))
            outputs(NI - 2, 0, False, lambda: chunk_states(NI - 1, 1, False))
            outputs(NI - 1, 1, False, lambda: None)

            def x2(k):
                pe.wait_ge(S[f"cT_in{k % 2}"], 16 * (k // 2 + 1))
                if k:
                    pe.wait_ge(S["c_gate"], NH * k)
                else:
                    pe.wait_ge(S["b_evac"], 2 * NI)
                for h in range(NH):
                    last = mm(bank[h][:, :], w_in[:, DI + h * P:DI + (h + 1) * P], xT_sb[k % 2], start=True, stop=True)
                last.then_inc(S["c_x2"], 1)

            def project(k):
                pe.wait_ge(S["c_mul"], NH * (k + 1))
                if k >= 2:
                    pe.wait_ge(S["c_r"], k - 1)
                for j in range(TB):
                    for h in range(NH):
                        last = mm(bank[2 + k % 2][:, j * P:(j + 1) * P], yT[k % 3][h].rearrange("p (m j) -> p j m", j=TB)[:, j, :],
                                  w_out[:, h, :], start=(h == 0), stop=(h == NH - 1))
                last.then_inc(S["c_out"], 1)

            def turn_z(k):
                pe.wait_ge(S["c_z"], TB * (k + 1))
                if k >= 2:
                    pe.wait_ge(S["c_hT"], k - 1)
                for j in range(TB):
                    last = nc.tensor.transpose(bank[4 + k % 2][:, j * P:(j + 1) * P], z_rows[:, TB * k + j, 0:DM],
                                               ident[:, :])
                last.then_inc(S["c_zt"], 1)

            def route(k):
                pe.wait_ge(S["c_hT"], k + 1)
                if k:
                    pe.wait_ge(S["c_lg"], k)
                for j in range(TB):
                    last = mm(bank[6][:, NE * j:NE * (j + 1)], hT[:, k, j * P:(j + 1) * P], w_rt[:, :],
                              start=True, stop=True)
                last.then_inc(S["c_l"], 1)

            x2(0)
            x2(1)
            for k in range(NBLK + 3):
                if k < NBLK:
                    project(k)
                if k + 2 < NBLK:
                    x2(k + 2)
                if 2 <= k < NBLK + 2:
                    turn_z(k - 2)
                if k >= 3:
                    route(k - 3)

            pe.wait_ge(S["r_dve"], 9)
            pe.wait_ge(S["r_cst"], 8)
            mm(bank[7][:, :], tri, rt[1].rearrange("p e t -> p (e t)"), start=True, stop=True)
            mm(bank[5][:, :], ones, rt[1].rearrange("p e t -> p (e t)"), start=True, stop=True).then_inc(S["r_pe"], 1)

            tv = tern[:, :]
            for g in range(9):
                pe.wait_ge(S["w_q"], 14)
                if g >= 2:
                    pe.wait_ge(S["w_c"], g - 1)
                for m in range(4):
                    n = 4 * g + m
                    last = nc.tensor.transpose(bank[2 + g % 2][:, m * P:(m + 1) * P], tv[:, n * P:(n + 1) * P], ident[:, :])
                last.then_inc(S["w_t"], 1)

            pe.wait_ge(S["w_c"], 9)

            def up(k):
                if k >= 2:
                    pe.wait_ge(S["s_act"], FH * (k - 1))
                for h in range(FH):
                    last = mm(bank[2 * (k % 2) + h][:, :], w1T[:, h * P:(h + 1) * P], hT[:, k, :], start=True, stop=True)
                last.then_inc(S["s_up"], 1)

            def down(k):
                pe.wait_ge(S["s_act"], FH * (k + 1))
                if k >= 2:
                    pe.wait_ge(S["s_add"], k - 1)
                elif k == 1:
                    pe.wait_ge(S["r_dve"], 13)
                for j in range(TB):
                    for h in range(FH):
                        last = mm(bank[4 + k % 2][:, j * P:(j + 1) * P], h1[k % 2][h][:, j * P:(j + 1) * P],
                                  w2T[:, h * P:(h + 1) * P], start=(h == 0), stop=(h == FH - 1))
                last.then_inc(S["s_dn"], 1)

            up(0)
            for k in range(NBLK):
                if k + 1 < NBLK:
                    up(k + 1)
                down(k)

            pe.wait_ge(S["s_act"], FH * NBLK)
            pe.wait_ge(S["s_add"], NBLK)
            pe.wait_ge(S["r_dve"], R_LAST)

            def known(v):
                return isinstance(v, int)

            def turn(j, q, r):
                pe.wait_ge(S[f"d_in{r // 4}"], (q + 1) * 16)
                if not (known(j) and j < 2):
                    pe.wait_ge(S["d_h"], j - 1)
                nc.tensor.transpose(bank[r % 2][:, 0:P], zt[r][:, 0:DM], ident[:, :]).then_inc(S["d_t"], 1)

            def expert_up(j, r):
                pe.wait_ge(S["d_h"], j + 1)
                pe.wait_ge(S["d_w"], j + 1)
                if not (known(j) and j < 2):
                    pe.wait_ge(S["d_act"], j - 1)
                for h in range(FH):
                    last = mm(bank[2 + r % 2][:, h * P:(h + 1) * P], w1s[r % 4][:, h * P:(h + 1) * P], hb[r % 4],
                              start=True, stop=True)
                last.then_inc(S["d_up"], 1)

            def expert_down(j, r):
                e = pe.value_load(tile_expert[0:1, bass.ds(j, 1)], min_val=0, max_val=NE - 1)
                pe.wait_ge(S["d_act"], j + 1)
                if not (known(j) and j < 2):
                    pe.wait_ge(S["d_y"], j - 1)
                for h in range(FH):
                    last = mm(bank[4 + r % 2][:, 0:DM], ab[r % 4][:, h * P:(h + 1) * P],
                              w2T[:, bass.ds(e * FF + (FF + h * P), DM)], start=(h == 0), stop=(h == FH - 1))
                last.then_inc(S["d_o"], 1)

            def pe_steps(j0, q, first=False):
                for r in range(GRP):
                    turn(j0 + r, q, r)
                    if not first or r >= 2:
                        expert_up(j0 + (r - 2), (r - 2) % GRP)
                    if not first or r >= 4:
                        expert_down(j0 + (r - 4), (r - 4) % GRP)

            pe_steps(0, 0, first=True)
            with pe.Fori(1, SLOT_TILES // GRP) as q:
                pe_steps(q * GRP, q)
            n = SLOT_TILES
            for m in range(4):
                if m < 2:
                    expert_up(n - 2 + m, GRP - 2 + m)
                expert_down(n - 4 + m, GRP - 4 + m)

        @block.scalar
        def _(act):
            af = nc.scalar.activation
            act.wait_ge(S["params_in"], 16 * NPAR)
            af(dt_, logdt, ACT.Exp).then_inc(S["tb_act"], 1)
            af(aexp, alog, ACT.Exp).then_inc(S["tb_act"], 1)
            act.wait_ge(S["tb_dve"], 6)
            af(pw, pw, ACT.Exp).then_inc(S["tb_act"], 1)
            def evac(k):
                act.wait_ge(S["a_mm"], k + 1)
                if k >= 2:
                    act.wait_ge(S["a_conv"], 6 * (k - 1))
                if k >= 3:
                    act.wait_ge(S["a_tr"], NH * (k - 2))
                for h in range(NH):
                    ps = bank[2 * (k % 2) + h][:, :]
                    af(x1p[k % 2][h][:, :, TAPS - 1:], ps.rearrange("p (b t) -> p b t", b=BB), ACT.Identity,
                       bias=in_b_sb[:, h:h + 1]).then_inc(S["a_evac"], 1)
                    af(acc[k % 3][h], ps, ACT.Identity, bias=tap_bias[:, h:h + 1],
                       scale=conv_w_sb[:, h, TAPS - 1:TAPS]).then_inc(S["a_evac"], 1)

            act.wait_ge(S["consts"], 8)
            act.wait_ge(S["tb_dve"], 7)
            evac(0)
            act.wait_ge(S["tb_zero_dve"], 1)
            act.wait_ge(S["tb_dve"], TB_TR)
            for h in range(NH):
                for q in range(4):
                    rows = slice(32 * q, 32 * q + 32)
                    af(toep[rows, h, :, 32 * q:32 * q + 32],
                       ttr[rows, h, :, :].rearrange("p t i -> p i t")[:, :, ::-1],
                       ACT.Copy).then_inc(S["tb_place_act"], 1)

            for k in range(NBLK):
                if k + 1 < NBLK:
                    evac(k + 1)
                act.wait_ge(S["a_conv"], 6 * (k + 1))
                for h in range(NH):
                    af(acc[k % 3][h], acc[k % 3][h], ACT.Silu).then_inc(S["a_silu"], 1)

            def b_evac(i, r):
                act.wait_ge(S["b_y"], i + 1)
                for h in range(NH):
                    af(u_all[:, h, bass.ds(i, 1), :].rearrange("p a m -> p (a m)"), bank[2 * r + h][:, 0:NC],
                       ACT.Copy).then_inc(S["b_evac"], 1)

            with act.Fori(0, NI // 2) as j:
                b_evac(j * 2, 0)
                b_evac(j * 2 + 1, 1)

            def gates(k):
                act.wait_ge(S["c_x2"], k + 1)
                if k >= 2:
                    act.wait_ge(S["c_mul"], NH * (k - 1))
                elif k == 0:
                    act.wait_ge(S["b_y"], NI)
                    act.wait_ge(S["fill_in"], 16 * (SLOT_TILES // FILL + 1))
                for h in range(NH):
                    af(gate[k % 2][h], bank[h][:, :], ACT.Silu, bias=in_b_sb[:, 2 + h:3 + h]).then_inc(S["c_gate"], 1)

            def norm_T(k):
                act.wait_ge(S["c_zt"], k + 1)
                af(hT[:, k, :], bank[4 + k % 2][:, :], ACT.Identity, bias=bet, scale=gam).then_inc(S["c_hT"], 1)

            def ffn_norm(k):
                act.wait_ge(S["c_xn"], TB * (k + 1))
                if k == 0:
                    act.wait_ge(S["r_cst"], 1)
                for j in range(TB):
                    af(z_rows[:, TB * k + j, 0:DM], xn[:, TB * k + j, :], ACT.Copy,
                       scale=rs[k % 2][:, 4, j:j + 1]).then_inc(S["c_z"], 1)

            gates(0)
            gates(1)
            for k in range(NBLK + 2):
                if 1 <= k <= NBLK:
                    ffn_norm(k - 1)
                if k + 2 < NBLK:
                    gates(k + 2)
                if 2 <= k:
                    norm_T(k - 2)

            act.wait_ge(S["r_dve"], 2)
            af(rt[0], rt[0], ACT.Exp).then_inc(S["r_exp"], 1)

            for g in range(9):
                act.wait_ge(S["w_t"], g + 1)
                both = u_reg[:, 2 * GW:4 * GW]
                af(both[:, 512 * g:512 * (g + 1)], bank[2 + g % 2][:, :], ACT.Copy).then_inc(S["w_c"], 1)

            for k in range(NBLK):
                act.wait_ge(S["s_up"], k + 1)
                if k >= 2:
                    act.wait_ge(S["s_dn"], k - 1)
                for h in range(FH):
                    af(h1[k % 2][h], bank[2 * (k % 2) + h][:, :], ACT.Silu).then_inc(S["s_act"], 1)

            def known(v):
                return isinstance(v, int)

            def d_norm(j, r):
                act.wait_ge(S["d_t"], j + 1)
                if not (known(j) and j < 4):
                    act.wait_ge(S["d_up"], j - 3)
                af(hb[r % 4], bank[r % 2][:, 0:P], ACT.Identity, bias=bet, scale=gam).then_inc(S["d_h"], 1)

            def d_silu(j, r):
                act.wait_ge(S["d_up"], j + 1)
                if not (known(j) and j < 4):
                    act.wait_ge(S["d_o"], j - 3)
                af(ab[r % 4], bank[2 + r % 2][:, 0:FF], ACT.Silu).then_inc(S["d_act"], 1)

            def act_steps(j0, first=False):
                for r in range(GRP):
                    d_norm(j0 + r, r)
                    if not first or r >= 2:
                        d_silu(j0 + (r - 2), (r - 2) % GRP)

            act.wait_ge(S["r_dve"], R_LAST)
            act_steps(0, first=True)
            with act.Fori(1, SLOT_TILES // GRP) as q:
                act_steps(q * GRP)
            d_silu(SLOT_TILES - 2, GRP - 2)
            d_silu(SLOT_TILES - 1, GRP - 1)

            for k in range(NBLK):
                act.wait_ge(S["e_rs"], k + 1)
                if k >= 3:
                    act.wait_ge(S[f"e_out{k % 3}"], 16 * (k // 3))
                for j in range(TB):
                    af(ob[k % 3][:, j, :], yb[k % 4][:, j, :], ACT.Identity, bias=rs[k % 2][:, 3, j:j + 1],
                       scale=rs[k % 2][:, 1, j:j + 1]).then_inc(S["e_n"], 1)

        @block.vector
        def _(dve):
            v = nc.vector
            n_tb = [0]

            def table(ins):
                ins.then_inc(S["tb_dve"], 1)
                n_tb[0] += 1

            def settled():
                dve.wait_ge(S["tb_dve"], n_tb[0])

            v.memset(toep, 0.0).then_inc(S["tb_zero_dve"], 1)
            v.memset(enter, 0.0).then_inc(S["tb_zero_dve"], 1)
            dve.wait_ge(S["params_in"], 16 * NPAR)
            table(v.tensor_tensor(tap_bias, in_b_sb[:, 0:NH], conv_w_sb[:, :, TAPS - 1], ALU.mult))
            dve.wait_ge(S["tb_act"], 2)
            dtb = dt_.rearrange("p (h a) -> p h a", a=1).broadcast_to([P, NH, NST])
            table(v.tensor_tensor(a_, aexp, dtb, ALU.mult))
            table(v.tensor_tensor(db, bpar, dtb, ALU.mult))
            settled()
            table(v.tensor_tensor(wk, db, cpar, ALU.mult))
            dve.wait_ge(S["consts"], 8)

            def wide(ap):
                return ap.rearrange("p h n -> p (h n)").rearrange("p (m a) -> p m a", a=1).broadcast_to([P, NH * NST, L])

            def times(ap):
                return ap.rearrange("p (a t) -> p a t", a=1).broadcast_to([P, NH * NST, L])

            def flat(ap):
                return ap.rearrange("p h n t -> p (h n) t")

            table(v.tensor_tensor(flat(pw_r), wide(a_), times(t_rev), ALU.mult))
            table(v.tensor_tensor(flat(pw_f), wide(a_), times(t_fwd), ALU.mult))
            dve.wait_ge(S["tb_act"], 3)
            table(v.tensor_tensor(tap_bias, tap_bias, conv_b_sb, ALU.add))
            table(v.tensor_tensor(flat(esrc), flat(pw_r), wide(db), ALU.mult))
            table(v.tensor_tensor(flat(ksrc), flat(pw_r), wide(wk), ALU.mult))
            dve.wait_ge(S["tb_zero"], 2)
            for h in range(NH):
                table(v.tensor_tensor(osrc[:, h, :, 16 * h:16 * h + 16], pw_f[:, h, :, :].rearrange("p n t -> p t n"),
                                      cpar[:, h, :].rearrange("p (a n) -> p a n", a=1).broadcast_to([P, L, NST]), ALU.mult))
            table(v.tensor_copy(dsrc.rearrange("p (h n) -> p h n", h=NH), pw_f[:, :, :, L - 1]))
            settled()
            for h in range(NH):
                table(v.tensor_reduce(kpad[:, h, 0:L], ksrc[:, h, :, :].rearrange("p n t -> p t n"), AX.X, ALU.add))
                table(v.transpose(etr[:, h, :, :].rearrange("p n i -> p (n i)"), esrc[:, h, :, :].rearrange("p n t -> p (n t)")))
                table(v.transpose(otr[:, h, :, :].rearrange("p t i -> p (t i)"), osrc[:, h, :, :].rearrange("p t s -> p (t s)")))
            table(v.transpose(decay[:, :], dsrc))
            settled()
            for h in range(NH):
                table(v.transpose(ttr[:, h, :, :], windows[h]))
            assert n_tb[0] == TB_TR, n_tb[0]
            settled()
            dve.wait_ge(S["tb_zero_dve"], 2)
            for h in range(NH):
                for q in range(4):
                    rows = slice(32 * q, 32 * q + 32)
                    v.tensor_copy(enter[rows, h, :, 32 * q + 16 * h:32 * q + 16 * h + 16],
                                  etr[rows, h, :, :].rearrange("p n i -> p i n")).then_inc(S["tb_place_dve"], 1)

            def conv(k):
                dve.wait_ge(S["a_evac"], 4 * (k + 1))
                for n, tap in enumerate((2, 1, 0)):
                    for h in range(NH):
                        if n:
                            dve.wait_ge(S["a_conv"], 6 * k + 2 * (n - 1) + h + 1)
                        av = acc[k % 3][h].rearrange("p (b t) -> p b t", b=BB)
                        v.scalar_tensor_tensor(out=av, in0=x1p[k % 2][h][:, :, tap:tap + SEQ],
                                               scalar=conv_w_sb[:, h, tap:tap + 1], in1=av, op0=ALU.mult,
                                               op1=ALU.add).then_inc(S["a_conv"], 1)

            def spread(k):
                dve.wait_ge(S["a_silu"], NH * (k + 1))
                if k == 0:
                    dve.wait_ge(S["tb_place_dve"], 8)
                    dve.wait_ge(S["tb_place_act"], 8)
                for h in range(NH):
                    v.transpose(u_all[:, h, :, CB * k:CB * (k + 1)].rearrange("p i c -> p c i"),
                                acc[k % 3][h].rearrange("p (c t) -> p c t", t=L)).then_inc(S["a_tr"], 1)

            conv(0)
            for k in range(NBLK):
                if k + 1 < NBLK:
                    conv(k + 1)
                spread(k)

            def scan(i, r, peel):
                dve.wait_ge(S["b_s"], i + 1)
                dve.wait_ge(S["b_d0"], i + 1)
                if not peel:
                    dve.wait_ge(S["b_y"], i - 1)
                v.tensor_tensor_scan(states[r], decay_row[r], bank[4 + r][:, 0:NC], 0.0, ALU.mult,
                                     ALU.add).then_inc(S["b_h"], 1)

            scan(0, 0, True)
            scan(1, 1, True)
            with dve.Fori(1, NI // 2) as j:
                scan(j * 2, 0, False)
                scan(j * 2 + 1, 1, False)

            def gather(k):
                if k == 0:
                    dve.wait_ge(S["b_evac"], 2 * NI)
                    dve.wait_ge(S["fill_in"], 16 * (SLOT_TILES // FILL + 1))
                if k >= 3:
                    dve.wait_ge(S["c_out"], k - 2)
                for h in range(NH):
                    v.transpose(yT[k % 3][h].rearrange("p (c t) -> p c t", t=L),
                                u_all[:, h, :, CB * k:CB * (k + 1)].rearrange("p i c -> p c i")).then_inc(S["c_ytr"], 1)

            def residual(k):
                dve.wait_ge(S["c_out"], k + 1)
                dve.wait_ge(S["c_xb"], k + 1)
                if k >= 2:
                    dve.wait_ge(S["c_xn"], TB * (k - 1))
                v.tensor_tensor(res[k % 2], bank[2 + k % 2][:, :].rearrange("p (j d) -> p j d", j=TB),
                                x_in[k % 2], ALU.add).then_inc(S["c_r"], 1)
                dve.wait_ge(S["c_r"], k + 1)
                for j in range(TB):
                    v.bn_stats(stats[k % 2][:, j, :], res[k % 2][:, j, :]).then_inc(S["c_st"], 1)
                if k >= 2:
                    dve.wait_ge(S["c_rs"], k - 1)
                for j in range(TB):
                    dve.wait_ge(S["c_st"], TB * k + j + 1)
                    v.bn_aggr(mv[k % 2][:, j, :], stats[k % 2][:, j, :]).then_inc(S["c_ag"], 1)

            def normalise(k):
                dve.wait_ge(S["c_rs"], k + 1)
                for j in range(TB):
                    v.tensor_scalar(xn[:, TB * k + j, :], res[k % 2][:, j, :], mv[k % 2][:, j, 0:1],
                                    rs[k % 2][:, 1, j:j + 1], ALU.subtract, ALU.mult).then_inc(S["c_xn"], 1)

            def keep_logits(k):
                dve.wait_ge(S["c_l"], k + 1)
                v.tensor_copy(logits[:, :, TB * k:TB * (k + 1)].rearrange("p e j -> p j e"),
                              bank[6][:, 0:TB * NE].rearrange("p (j e) -> p j e", e=NE)).then_inc(S["c_lg"], 1)

            gather(0)
            gather(1)
            for k in range(NBLK + 4):
                if k + 2 < NBLK:
                    gather(k + 2)
                if k < NBLK:
                    residual(k)
                if 1 <= k <= NBLK:
                    normalise(k - 1)
                if k >= 4:
                    keep_logits(k - 4)

            n_r = [0]

            def r_step(ins):
                ins.then_inc(S["r_dve"], 1)
                n_r[0] += 1
                dve.wait_ge(S["r_dve"], n_r[0])

            dve.wait_ge(S["c_lg"], NBLK)
            dve.wait_ge(S["r_cst"], 8)
            dve.wait_ge(S["c_out"], NBLK)
            mx = rsm[:, 0:64]
            best = rsm[:, 64:128]
            cnt = rsm[:, 128:136]
            cnt_i = rsm[:, 136:144].bitcast(I32)
            tiles = rsm[:, 144:152]
            upto = rsm[:, 152:160]
            base = rsm[:, 160:168]
            w8 = rsm[:, 168:176]
            one8 = rsm[:, 176:184]
            sumexp = rsm[:, 192:256]
            posf = rsm[:, 256:320]
            slot_lo = rsm[:, 480:544].bitcast(I32)
            slot_hi = rsm[:, 544:608].bitcast(I32)
            jf = rsm[:, 320:320 + SLOT_TILES]
            ef = rsm[:, 400:400 + SLOT_TILES]

            def over_t(ap):
                return ap.rearrange("p (e a) -> p e a", a=1).broadcast_to([P, NE, NT])

            def over_e(ap):
                return ap.rearrange("p (a t) -> p a t", a=1).broadcast_to([P, NE, NT])

            def by_t(ap):
                return ap.rearrange("p e t -> p t e")

            r_step(v.tensor_reduce(mx, by_t(logits[:, :, :]), AX.X, ALU.max))
            r_step(v.tensor_tensor(rt[0], logits[:, :, :], over_e(mx), ALU.subtract))
            r_step(v.tensor_tensor(rt[1], logits[:, :, :], over_e(mx), ALU.is_equal))
            r_step(v.tensor_tensor(rt[1], rt[1], over_t(w8), ALU.mult))
            r_step(v.tensor_reduce(best, by_t(rt[1]), AX.X, ALU.max))
            r_step(v.tensor_copy(rt[2], over_t(w8)))
            dve.wait_ge(S["r_exp"], 1)
            r_step(v.tensor_reduce(sumexp, by_t(rt[0]), AX.X, ALU.add))
            r_step(v.reciprocal(top_p[:, :], sumexp))
            r_step(v.tensor_tensor(rt[1], rt[2], over_e(best), ALU.is_equal))
            dve.wait_ge(S["r_pe"], 1)
            r_step(v.tensor_copy(rt[2], bank[5][:, :].rearrange("p (e t) -> p e t", e=NE)))
            r_step(v.tensor_tensor_scan(rt[3].rearrange("p e t -> p (e t)"), lead_mask.rearrange("p e t -> p (e t)"),
                                        rt[2].rearrange("p e t -> p (e t)"), 0.0, ALU.mult, ALU.add))
            r_step(v.tensor_tensor(rt[4], rt[3], rt[2], ALU.subtract))
            r_step(v.tensor_tensor(rt[4], bank[7][:, :].rearrange("p (e t) -> p e t", e=NE), rt[4], ALU.add))
            r_step(v.tensor_scalar(cnt, rt[3][:, :, NT - 1], float(P - 1), None, ALU.add))
            r_step(v.tensor_copy(cnt_i, cnt))
            r_step(v.tensor_scalar(cnt_i, cnt_i, 7, None, ALU.arith_shift_right))
            r_step(v.tensor_copy(tiles, cnt_i))
            r_step(v.tensor_tensor_scan(upto, one8, tiles, 0.0, ALU.mult, ALU.add))
            r_step(v.tensor_tensor(base, upto, tiles, ALU.subtract))
            r_step(v.tensor_scalar(base, base, float(P), None, ALU.mult))
            r_step(v.tensor_tensor(rt[4], rt[4], over_t(base), ALU.add))
            r_step(v.tensor_tensor(rt[4], rt[4], rt[1], ALU.mult))
            r_step(v.tensor_reduce(posf, by_t(rt[4]), AX.X, ALU.add))
            r_step(v.tensor_copy(slot[:, :], posf))
            r_step(v.tensor_scalar(slot_lo, slot[:, :], P - 1, None, ALU.bitwise_and))
            r_step(v.tensor_scalar(slot_hi, slot[:, :], 7, None, ALU.arith_shift_right))
            r_step(v.tensor_copy(posf, slot_lo))
            r_step(v.tensor_copy(sumexp, slot_hi))
            r_step(v.scalar_tensor_tensor(out=slot[:, :], in0=posf, scalar=float(SLOT_TILES), in1=sumexp,
                                          op0=ALU.mult, op1=ALU.add))
            ej = work[:, 4096:4096 + SLOT_TILES * NE].rearrange("p (j e) -> p j e", e=NE)
            r_step(v.tensor_tensor(ej, jf.rearrange("p (j a) -> p j a", a=1).broadcast_to([P, SLOT_TILES, NE]),
                                   upto.rearrange("p (a e) -> p a e", a=1).broadcast_to([P, SLOT_TILES, NE]), ALU.is_ge))
            r_step(v.tensor_reduce(ef, ej, AX.X, ALU.add))
            r_step(v.tensor_scalar(ef, ef, float(NE - 1), None, ALU.min))
            r_step(v.tensor_copy(tile_expert[:, :], ef))
            assert n_r[0] == R_LAST, n_r[0]

            n_w = [0]

            def w_step(ins):
                ins.then_inc(S["w_q"], 1)
                n_w[0] += 1
                dve.wait_ge(S["w_q"], n_w[0])

            dve.wait_ge(S["w_in"], 16 * (NE + 3))
            w_step(v.tensor_reduce(scale1, nat1.rearrange("p (r d) -> p r d", d=DM), AX.X, ALU.add, apply_absolute_value=True))
            w_step(v.tensor_reduce(scale2, nat2.rearrange("p (r f) -> p r f", f=FF), AX.X, ALU.add, apply_absolute_value=True))
            w_step(v.tensor_scalar(scale1, scale1, 1.0 / DM, EPS, ALU.mult, ALU.max))
            w_step(v.tensor_scalar(scale2, scale2, 1.0 / FF, EPS, ALU.mult, ALU.max))
            w_step(v.tensor_scalar(hs12, s12, 0.5, None, ALU.mult))
            w_step(v.tensor_scalar(nhs12, s12, -0.5, None, ALU.mult))
            for nat, lo, n, wd, to in ((nat1, 0, 18, DM, 0), (nat2, 18, 9, FF, GW)):
                def per_row(ap):
                    return ap[:, lo:lo + n].rearrange("p (r a) -> p r a", a=1).broadcast_to([P, n, wd])
                nv = nat.rearrange("p (r d) -> p r d", d=wd)
                tv = tern[:, to:to + GW].rearrange("p (r d) -> p r d", d=wd)
                w_step(v.tensor_tensor(tv, nv, per_row(hs12), ALU.is_gt))
                w_step(v.tensor_tensor(nv, nv, per_row(nhs12), ALU.is_lt))
                w_step(v.tensor_tensor(tv, tv, nv, ALU.subtract))
                w_step(v.tensor_tensor(tv, tv, per_row(s12), ALU.mult))

            for k in range(NBLK):
                dve.wait_ge(S["s_dn"], k + 1)
                xv = xn[:, TB * k:TB * (k + 1), :]
                v.tensor_tensor(xv, bank[4 + k % 2][:, :].rearrange("p (j d) -> p j d", j=TB), xv,
                                ALU.add).then_inc(S["s_add"], 1)

            def known(x_):
                return isinstance(x_, int)

            def fetch(j, q, r):
                e = dve.value_load(tile_expert[0:1, bass.ds(j, 1)], min_val=0, max_val=NE - 1)
                if not (known(j) and j < 4):
                    dve.wait_ge(S["d_up"], j - 3)
                v.tensor_copy(w1s[r % 4], w1T[:, bass.ds(e * FF + FF, FF)]).then_inc(S["d_w"], 1)
                if r % 4 == 0:
                    dve.wait_ge(S[f"d_in{r // 4}"], (q + 1) * 16)
                    if not (known(q) and q == 0):
                        for m in range(4):
                            dve.wait_ge(S[f"d_sc{r + m}"], q * 16)
                    v.tensor_copy(ids[:, r:r + 4], z_rows[:, r:r + 4, DM:ROW].bitcast(I32)
                                  .rearrange("p t a -> p (t a)")).then_inc(S["d_id"], 1)

            def d_rows(j, q, r):
                dve.wait_ge(S["d_o"], j + 1)
                if not (known(q) and q == 0):
                    dve.wait_ge(S[f"d_sc{r}"], q * 16)
                v.tensor_copy(yt[r], bank[4 + r % 2][:, 0:DM]).then_inc(S["d_y"], 1)

            def dve_steps(j0, q, first=False):
                for r in range(GRP):
                    fetch(j0 + r, q, r)
                    if r >= 4:
                        d_rows(j0 + (r - 4), q, r - 4)
                    elif not first:
                        d_rows(j0 + (r - 4), q - 1, r + 4)

            dve_steps(0, 0, first=True)
            dve_steps(GRP, 1)
            with dve.Fori(2, SLOT_TILES // GRP) as q:
                dve_steps(q * GRP, q)
            for m in range(4):
                d_rows(SLOT_TILES - 4 + m, SLOT_TILES // GRP - 1, 4 + m)

            def e_sum(k):
                dve.wait_ge(S[f"e_in{k % 4}"], 16 * (k // 4 + 1))
                for j in range(TB):
                    v.scalar_tensor_tensor(out=yb[k % 4][:, j, :], in0=yb[k % 4][:, j, :],
                                           scalar=top_p[:, TB * k + j:TB * k + j + 1], in1=xn[:, TB * k + j, :],
                                           op0=ALU.mult, op1=ALU.add).then_inc(S["e_y"], 1)
                if k >= 2:
                    dve.wait_ge(S["e_rs"], k - 1)
                for j in range(TB):
                    dve.wait_ge(S["e_y"], TB * k + j + 1)
                    v.bn_stats(stats[k % 2][:, j, :], yb[k % 4][:, j, :]).then_inc(S["e_st"], 1)
                for j in range(TB):
                    dve.wait_ge(S["e_st"], TB * k + j + 1)
                    v.bn_aggr(mv[k % 2][:, j, :], stats[k % 2][:, j, :]).then_inc(S["e_ag"], 1)

            for k in range(NBLK):
                e_sum(k)

        @block.gpsimd
        def _(pool):
            g = nc.gpsimd
            g.dma_start(outb[:, :], out_b.rearrange("(a d) -> a d", a=1).broadcast_to([P, DM])).then_inc(S["fill_in"], 16)
            g.memset(work[:, 1024:3096], 0.0).then_inc(S["consts"], 1)
            g.iota(t_rev, pattern=[[-1, L]], base=L - 1, channel_multiplier=0,
                   allow_small_or_imprecise_dtypes=True).then_inc(S["consts"], 1)
            g.iota(t_fwd, pattern=[[1, L]], base=1, channel_multiplier=0,
                   allow_small_or_imprecise_dtypes=True).then_inc(S["consts"], 1)
            g.memset(ident[:, :], 0.0).then_inc(S["consts"], 1)
            g.memset(first_mask[:, :, :], 1.0).then_inc(S["consts"], 1)
            g.memset(half_neg[:, :], -0.5).then_inc(S["consts"], 1)
            pool.wait_ge(S["consts"], 6)
            g.memset(first_mask[:, :, 0:1], 0.0).then_inc(S["consts"], 1)
            g.affine_select(out=ident[:, :], in_=ident[:, :], compare_op=ALU.not_equal, fill=1.0, base=0,
                            pattern=[[-1, P]], channel_multiplier=1).then_inc(S["consts"], 1)
            for ap in (kpad, osrc, leave):
                g.memset(ap, 0.0).then_inc(S["tb_zero"], 1)
            pool.wait_ge(S["tb_zero"], 3)
            pool.wait_ge(S["tb_dve"], TB_TR)
            for h in range(NH):
                for q in range(4):
                    rows = slice(32 * q, 32 * q + 32)
                    g.tensor_copy(leave[rows, h, :, 32 * q:32 * q + 32],
                                  otr[rows, h, :, :].rearrange("p t i -> p i t")).then_inc(S["tb_place_pool"], 1)
                    pool.wait_ge(S["tb_place_pool"], 4 * h + q + 1)

            def multipliers(i, r, peel):
                if not peel:
                    pool.wait_ge(S["b_h"], i - 1)
                g.tensor_tensor(decay_row[r], first_mask[:, :, :].rearrange("p b c -> p (b c)"),
                                decay[:, bass.ds(i, 1)].broadcast_to([P, NC]), ALU.mult).then_inc(S["b_d0"], 1)

            pool.wait_ge(S["a_tr"], NH * NBLK)
            pool.wait_ge(S["consts"], 8)
            multipliers(0, 0, True)
            multipliers(1, 1, True)
            with pool.Fori(1, NI // 2) as j:
                multipliers(j * 2, 0, False)
                multipliers(j * 2 + 1, 1, False)

            g.memset(work[:, 2048:2048 + FILL * ROW], 0.0).then_inc(S["unused"], 1)
            sorted_fill = sorted_rows.rearrange("(p n j) w -> n p j w", j=FILL, p=P)
            for n in range(SLOT_TILES // FILL):
                pool.wait_ge(S["unused"], n + 1)
                pool.wait_ge(S["fill_in"], 16 * (n + 1))
                g.iota(fill[:, :, DM:ROW].bitcast(I32).rearrange("p j a -> p (j a)"), pattern=[[1, FILL]],
                       base=TOK + n * FILL, channel_multiplier=SLOT_TILES).then_inc(S["unused"], 1)
                pool.wait_ge(S["unused"], n + 2)
                g.dma_start(sorted_fill[n], fill).then_inc(S["fill_in"], 16)
            pool.wait_ge(S["fill_in"], 16 * (SLOT_TILES // FILL + 1))

            def multiply(k):
                pool.wait_ge(S["c_gate"], NH * (k + 1))
                pool.wait_ge(S["c_ytr"], NH * (k + 1))
                for h in range(NH):
                    g.tensor_tensor(yT[k % 3][h], yT[k % 3][h], gate[k % 2][h], ALU.mult).then_inc(S["c_mul"], 1)
                pool.wait_ge(S[f"x_in{k % 2}s"], 16 * (k // 2 + 1))
                g.tensor_tensor(x_in[k % 2], x_in[k % 2],
                                outb[:, :].rearrange("p (a d) -> p a d", a=1).broadcast_to([P, TB, DM]),
                                ALU.add).then_inc(S["c_xb"], 1)

            n_p = [0]
            pool_chain = sem("pool_chain")

            def chain(ins):
                ins.then_inc(pool_chain, 1)
                n_p[0] += 1
                pool.wait_ge(pool_chain, n_p[0])

            def rstd(k):
                pool.wait_ge(S["c_ag"], TB * (k + 1))
                if k >= 2:
                    pool.wait_ge(S["c_z"], TB * (k - 1))
                t, var = rs[k % 2], mv[k % 2][:, :, 1]
                chain(g.tensor_scalar(t[:, 0, :], var, EPS, None, ALU.add))
                chain(g.tensor_tensor(t[:, 1, :], t[:, 0, :], half_neg[:, :], ALU.pow))
                chain(g.tensor_tensor(t[:, 2, :], t[:, 1, :], t[:, 1, :], ALU.mult))
                chain(g.tensor_tensor(t[:, 3, :], t[:, 2, :], var, ALU.mult))
                chain(g.tensor_scalar(t[:, 3, :], t[:, 3, :], EPS, None, ALU.add))
                g.tensor_tensor(t[:, 4, :], t[:, 3, :], half_neg[:, :], ALU.pow).then_inc(S["c_rs"], 1)

            multiply(0)
            g.iota(z_rows[:, :, DM:ROW].bitcast(I32).rearrange("p t a -> p (t a)"), pattern=[[BLK, NBLK], [1, TB]], base=0,
                   channel_multiplier=TB).then_inc(S["r_cst"], 1)
            for k in range(NBLK):
                if k + 1 < NBLK:
                    multiply(k + 1)
                rstd(k)

            pool.wait_ge(S["c_z"], TB * NBLK)
            pool.wait_ge(S["c_out"], NBLK)
            g.memset(lead_mask, 1.0).then_inc(S["r_cst"], 1)
            g.memset(work[:, 3584:3840], 1.0).then_inc(S["r_cst"], 1)
            g.memset(rsm[:, 176:184], 1.0).then_inc(S["r_cst"], 1)
            g.iota(rsm[:, 168:176], pattern=[[-1, NE]], base=NE, channel_multiplier=0,
                   allow_small_or_imprecise_dtypes=True).then_inc(S["r_cst"], 1)
            g.iota(rsm[:, 320:320 + SLOT_TILES], pattern=[[1, SLOT_TILES]], base=0, channel_multiplier=0,
                   allow_small_or_imprecise_dtypes=True).then_inc(S["r_cst"], 1)
            pool.wait_ge(S["r_cst"], 6)
            g.memset(lead_mask[:, :, 0:1], 0.0).then_inc(S["r_cst"], 1)
            g.affine_select(out=tri, in_=tri, compare_op=ALU.is_gt, fill=0.0, base=0,
                            pattern=[[1, P]], channel_multiplier=-1).then_inc(S["r_cst"], 1)
            pool.wait_ge(S["fill_in"], 16 * (SLOT_TILES // FILL + 1))
            pool.wait_ge(S["r_dve"], 29)
            for t in range(NT):
                g.indirect_dma_start(sorted_rows, bass.IndirectOffsetOnAxis(ap=slot[:, t:t + 1], axis=0),
                                     z_rows[:, t, :], None).then_inc(S["scat"], 16)

            def scatter(j, r):
                pool.wait_ge(S["d_y"], j + 1)
                pool.wait_ge(S["d_id"], j // 4 + 1)
                g.indirect_dma_start(routed_out, bass.IndirectOffsetOnAxis(ap=ids[:, r:r + 1], axis=0),
                                     yt[r], None).then_inc(S[f"d_sc{r}"], 16)

            for j in range(SLOT_TILES):
                scatter(j, j % GRP)

            for k in range(NBLK):
                pool.wait_ge(S["e_ag"], TB * (k + 1))
                if k >= 2:
                    pool.wait_ge(S["e_n"], TB * (k - 1))
                t = rs[k % 2]
                chain(g.tensor_scalar(t[:, 0, :], mv[k % 2][:, :, 1], EPS, None, ALU.add))
                g.tensor_scalar(t[:, 2, :], mv[k % 2][:, :, 0], -1.0, None, ALU.mult).then_inc(pool_chain, 1)
                n_p[0] += 1
                chain(g.tensor_tensor(t[:, 1, :], t[:, 0, :], half_neg[:, :], ALU.pow))
                g.tensor_tensor(t[:, 3, :], t[:, 2, :], t[:, 1, :], ALU.mult).then_inc(S["e_rs"], 1)


TB_TR = 21
R_LAST = 33


def kernel(**inputs):
    import numpy as np
    import concourse.bacc as bacc
    from concourse.bass_utils import run_bass_kernel_spmd as run

    a = {k: np.asarray(v) for k, v in inputs.items()}
    rows = np.ascontiguousarray(a["L0_attn_x"].reshape(TOK, DM))

    def halves(w):
        return np.ascontiguousarray(np.moveaxis(w.reshape((-1, P) + w.shape[1:]), 0, 1))

    arrays = {
        "xT": np.ascontiguousarray(rows.T), "x": rows,
        "in_wT": np.ascontiguousarray(a["L0_attn_in_proj_w"].T), "in_b": halves(a["L0_attn_in_proj_b"]),
        "conv_w": halves(a["L0_attn_conv_w"].reshape(DI, TAPS)), "conv_b": halves(a["L0_attn_conv_b"]),
        "a_log": halves(a["L0_attn_A_log"]), "b_par": halves(a["L0_attn_B_param"]),
        "c_par": halves(a["L0_attn_C_param"]), "log_dt": halves(a["L0_attn_log_dt"]),
        "out_wT": halves(a["L0_attn_out_proj_w"].T), "out_b": a["L0_attn_out_proj_b"],
        "sw1": a["L0_ffn_shared_w1"], "sw2": a["L0_ffn_shared_w2"], "ew1": a["L0_ffn_expert_w1"],
        "ew2": a["L0_ffn_expert_w2"], "routerT": np.ascontiguousarray(a["L0_ffn_router_w"].T),
        "gamma": a["L0_ffn_ln_gamma"].reshape(DM, 1), "beta": a["L0_ffn_ln_beta"].reshape(DM, 1),
    }
    nc = bacc.Bacc("TRN2", target_bir_lowering=False, num_devices=1)
    args = [nc.dram_tensor(n, v.shape, F32, kind="ExternalInput").ap() for n, v in arrays.items()]
    out = nc.dram_tensor("out", (TOK, DM), F32, kind="ExternalOutput").ap()
    build(nc, *args, out)
    r = run(nc, [arrays], core_ids=[0])
    return r.results[0]["out"].reshape(BATCH, SEQ, DM)
```

```python
from contextlib import ExitStack

import concourse.bass as bass
from concourse import mybir

F32 = mybir.dt.float32
I32 = mybir.dt.int32
ALU = mybir.AluOpType
ACT = mybir.ActivationFunctionType
AX = mybir.AxisListType

P = 128
BATCH, SEQ, DM = 32, 256, 128
TOK = BATCH * SEQ
DI = 256
NH = DI // P
NST = 16
L = 32
CH = SEQ // L
NC = BATCH * CH
NI = 32
TAPS = 4
BLK = 512
NBLK = TOK // BLK
BB = BLK // SEQ
CB = BLK // L
TB = BLK // P
NT = TOK // P
NE = 8
FF = 256
FH = FF // P
ROW = DM + 1
HALVES = 2
HB = NBLK // HALVES
HT = NT // HALVES
ST = HT + NE
SLOT_TILES = HALVES * ST
EPS = 1e-5
RING = 16
LOAD = 4
YR = 8
FILL = ST // 2


def build(nc, xT, x, in_wT, in_w_nat, in_b, conv_w, conv_b, a_log, b_par, c_par, log_dt, out_wT, out_b,
          sw1, sw2, ew1, ew2, routerT, gamma, beta, out):
    sorted_rows = nc.dram_tensor("sorted_rows", (SLOT_TILES * P, ROW), F32).ap()
    routed_out = nc.dram_tensor("routed_out", (TOK + SLOT_TILES * P, DM), F32).ap()
    x_tiles = x.rearrange("(k p j) d -> k p j d", j=TB, p=P)
    out_tiles = out.rearrange("(k p j) d -> k p j d", j=TB, p=P)
    routed_tiles = routed_out[0:TOK, :].rearrange("(k p j) d -> k p j d", j=TB, p=P)
    sorted_slots = sorted_rows.rearrange("(j p) w -> p j w", p=P)

    with ExitStack() as ctx:
        def sb(name, shape, dt=F32):
            return ctx.enter_context(nc.sbuf_tensor(name, shape, dt))

        def sem(name):
            return ctx.enter_context(nc.semaphore(name))

        bank = [ctx.enter_context(nc.psum_tensor(f"bank{n}", [P, 512], F32)) for n in range(8)]

        u_reg = sb("u_reg", [P, NH * NI * NC])
        t_reg = sb("t_reg", [P, NT * ROW])
        e_reg = sb("e_reg", [P, NH * NI * P])
        o_reg = sb("o_reg", [P, NH * NI * P])
        work = sb("work", [P, 7200])

        u_all = u_reg[:, :].rearrange("p (a h i c) -> p a h i c", a=HALVES, h=NH, i=NI)
        toep = t_reg[:, 0:NH * NI * P].rearrange("p (h i m) -> p h i m", h=NH, i=NI)
        enter = e_reg[:, :].rearrange("p (h i m) -> p h i m", h=NH, i=NI)
        leave = o_reg[:, :].rearrange("p (h i m) -> p h i m", h=NH, i=NI)
        z_rows = t_reg[:, :].rearrange("p (t w) -> p t w", w=ROW)
        hT = o_reg[:, :].rearrange("p (k n) -> p k n", n=BLK)
        xn = e_reg[:, :].rearrange("p (t d) -> p t d", d=DM)

        def halved(b):
            return b[:, 0:NC].rearrange("p (a c) -> p a c", a=HALVES)

        xT_sb = [work[:, 512 * r:512 * r + 512] for r in range(2)]
        x1p = [[work[:, 1024 + 518 * (2 * r + h):1024 + 518 * (2 * r + h + 1)]
                .rearrange("p (b t) -> p b t", b=BB) for h in range(NH)] for r in range(2)]
        acc = [[work[:, 3100 + 512 * (2 * r + h):3100 + 512 * (2 * r + h + 1)] for h in range(NH)]
               for r in range(3)]
        tmp = [work[:, 6176 + 512 * h:6688 + 512 * h] for h in range(NH)]
        decay_row = [work[:, 1024 + 256 * r:1280 + 256 * r] for r in range(2)]
        states = [work[:, 1536 + 256 * r:1792 + 256 * r] for r in range(2)]
        gate = [[work[:, 1024 + 512 * (2 * r + h):1536 + 512 * (2 * r + h)] for h in range(NH)] for r in range(2)]
        yT = [[work[:, 3072 + 512 * (2 * r + h):3584 + 512 * (2 * r + h)] for h in range(NH)] for r in range(3)]
        late = sb("late", [P, 2048])
        x_in = [late[:, 512 * r:512 * r + 512].rearrange("p (j d) -> p j d", j=TB) for r in range(3)]
        res = [work[:, 6144 + 512 * r:6656 + 512 * r].rearrange("p (j d) -> p j d", j=TB) for r in range(2)]

        w_in = sb("w_in", [P, 2 * DI])
        w_out = sb("w_out", [P, NH, DM])
        w_rt = sb("w_rt", [P, NE])
        small = sb("small", [P, 16 + 64 + 64])
        in_b_sb = small[:, 0:4]
        conv_w_sb = small[:, 4:12].rearrange("p (h k) -> p h k", h=NH)
        conv_b_sb = small[:, 12:14]
        logdt = small[:, 14:16]
        alog = small[:, 16:48].rearrange("p (h n) -> p h n", h=NH)
        bpar = small[:, 48:80].rearrange("p (h n) -> p h n", h=NH)
        cpar = small[:, 80:112].rearrange("p (h n) -> p h n", h=NH)
        gam = small[:, 112:113]
        bet = small[:, 113:114]
        tap_bias = small[:, 114:116]
        outb = sb("outb", [P, DM])
        tile_no = sb("tile_no", [P, ST])
        ident = sb("ident", [P, P])
        decay = sb("decay", [P, NI])
        first_mask = sb("first_mask", [P, BATCH, CH])
        stats = [sb(f"stats{r}", [P, TB, 6]) for r in range(2)]
        mv = [sb(f"mv{r}", [P, TB, 2]) for r in range(2)]
        rs = [sb(f"rs{r}", [P, 6, TB]) for r in range(2)]
        rsd = [sb(f"rsd{r}", [P, 2, TB]) for r in range(2)]
        norm = [sb(f"norm{r}", [P, 3, TB]) for r in range(4)]
        half_neg = sb("half_neg", [P, 2 * TB])
        logits = sb("logits", [P, NE, NT])
        w_tap3 = logits[:, 0:4, :].rearrange("p e t -> p (e t)")
        top_p = sb("top_p", [P, NT])
        slot = sb("slot", [P, NT], I32)
        weights_at = sb("weights_at", [P, SLOT_TILES], I32)

        sc = u_reg
        dt_ = sc[:, 0:2]
        a_ = sc[:, 8:40].rearrange("p (h n) -> p h n", h=NH)
        db = sc[:, 40:72].rearrange("p (h n) -> p h n", h=NH)
        wk = sc[:, 72:104].rearrange("p (h n) -> p h n", h=NH)
        aexp = sc[:, 104:136].rearrange("p (h n) -> p h n", h=NH)
        t_rev = sc[:, 136:168]
        t_fwd = sc[:, 168:200]
        pw_r = sc[:, 256:1280].rearrange("p (h n t) -> p h n t", h=NH, n=NST)
        pw_f = sc[:, 1280:2304].rearrange("p (h n t) -> p h n t", h=NH, n=NST)
        pw = sc[:, 256:2304]
        esrc = sc[:, 2304:3328].rearrange("p (h n t) -> p h n t", h=NH, n=NST)
        ksrc = sc[:, 3328:4352].rearrange("p (h n t) -> p h n t", h=NH, n=NST)
        kpad = sc[:, 4352:4480].rearrange("p (h t) -> p h t", h=NH)
        windows = [bass.AP(sc[:, :].tensor, 4352 + 64 * h, [[NH * NI * NC, P], [1, L], [1, L]]) for h in range(NH)]
        osrc = sc[:, 4480:6528].rearrange("p (h t s) -> p h t s", h=NH, s=32)
        dsrc = sc[:, 6528:6560]
        w_nat = sc[:, 11328:11584].rearrange("p (h m) -> p h m", h=NH)
        ttr = sc[:, 8256:10304].rearrange("p (h t i) -> p h t i", h=NH, i=NI)
        etr = sc[:, 10304:11328].rearrange("p (h n i) -> p h n i", h=NH, i=NI)
        otr = late[:, :].rearrange("p (h t i) -> p h t i", h=NH, i=NI)

        GW = (1 + NE) * FF
        nat = [work[:, 4640:4640 + GW], t_reg[:, 0:GW]]
        tern = [e_reg[:, 4096:4096 + GW], o_reg[:, 4096:4096 + GW]]
        w1T = u_reg[:, 0:GW]
        w2T = u_reg[:, GW:2 * GW]
        scales = sb("scales", [P, 96])
        WR = [FH * (1 + NE), 1 + NE]
        WD = [DM, FF]
        scale = [scales[:, 0:18], scales[:, 18:27]]
        above = [scales[:, 32:50], scales[:, 50:59]]
        below = [scales[:, 64:82], scales[:, 82:91]]
        WC = 5
        h1 = [[u_reg[:, 8192 + 512 * (2 * r + h):8704 + 512 * (2 * r + h)] for h in range(FH)] for r in range(2)]

        def chunk(n, c):
            cols = slice(512 * c, min(512 * (c + 1), GW))
            return cols, slice(cols.start // WD[n], cols.stop // WD[n])

        def tern_row(r):
            return tern[0][:, DM * r:DM * (r + 1)] if r < WR[0] else tern[1][:, FF * (r - WR[0]):FF * (r - WR[0] + 1)]

        def tern_block(n):
            if n < WR[0]:
                return tern[0][:, P * n:P * (n + 1)], n
            return tern[1][:, P * (n - WR[0]):P * (n - WR[0] + 1)], WR[0] + (n - WR[0]) // 2

        route_scratch = [o_reg[:, (NBLK - 4) * BLK:], work[:, 0:2048]]
        rt = [[scr[:, 256 * n:256 * (n + 1)].rearrange("p (e t) -> p e t", e=NE) for n in range(4)] for scr in route_scratch]
        lead_mask = late[:, 1536:1792].rearrange("p (e t) -> p e t", e=NE)
        tri = late[:, 1792:1920]
        ones = late[:, 1920:2048]
        wide8 = sb("wide8", [P, NE, HT])
        one8 = work[:, 7176:7184]
        upto = [sb(f"upto{a}", [P, NE]) for a in range(HALVES)]
        zt = [z_rows[:, m, :] for m in range(RING)]
        ids = sb("ids", [P, RING], I32)
        hb = [work[:, 128 * r:128 * r + 128] for r in range(4)]
        ws = [u_reg[:, 10240 + 512 * r:10752 + 512 * r].rearrange("p (m f) -> p m f", m=2) for r in range(4)]
        ab = [work[:, 1536 + 256 * r:1792 + 256 * r] for r in range(4)]
        yt = [work[:, 2560 + 128 * r:2688 + 128 * r] for r in range(YR)]
        yb = [work[:, 3584 + 512 * r:4096 + 512 * r].rearrange("p (j d) -> p j d", j=TB) for r in range(4)]
        ob = [work[:, 5632 + 512 * r:6144 + 512 * r].rearrange("p (j d) -> p j d", j=TB) for r in range(3)]
        fill = work[:, 2048:2048 + FILL * ROW].rearrange("p (j w) -> p j w", w=ROW)

        S = {n: sem(n) for n in (
            "params_in", "params_late", "consts", "tb_act", "tb_dve", "w3_s", "w3_t", "w3_c", "a_tmp", "a_add", "tb_zero", "tb_zero_dve", "tb_place_act", "tb_place_dve", "tb_place_pool",
            "xT_in0", "xT_in1", "a_x1", "a_mm", "a_evac", "a_conv", "a_silu", "a_tr",
            "b_s", "b_y", "b_h", "b_d0", "b_evac",
            "x_in0s", "x_in1s", "x_in2s", "outb_in", "c_u", "cT_in0", "cT_in1", "c_x2", "c_gate", "c_ytr", "c_mul_p", "c_mul_v", "c_xb", "c_out", "c_r",
            "c_st", "c_ag", "c_rs", "c_xn", "c_z", "c_zt", "c_hT", "c_l",
            "r_dve", "r_exp", "r_pe", "r_cst", "fill_in", "unused", "scat0", "scat1",
            "w_in1", "w_in2", "w_q", "w_sub", "w_s", "w_t", "w_c", "p_sum", "s_up", "s_act", "s_dn", "s_add",
            "d_in0", "d_in1", "d_in2", "d_in3", "d_t", "d_h", "d_w", "d_id", "d_up", "d_act", "d_o", "d_y",
            *(f"d_sc{m}" for m in range(8)), "e_in0", "e_in1", "e_in2", "e_in3", "e_y", "e_st", "e_ag", "e_u", "e_pm", "e_py", "e_rs", "e_m", "e_n",
            "e_out0", "e_out1", "e_out2")}
        NPAR = 9
        block = ctx.enter_context(nc.Block())

        @block.sync
        def _(sp):
            for dst, src in ((logdt, log_dt), (alog, a_log), (bpar, b_par), (cpar, c_par), (w_nat, in_w_nat)):
                sp.dma_start(dst, src).then_inc(S["params_in"], 16)
            for k in range(NBLK):
                if k >= 2:
                    sp.wait_ge(S["a_mm"], k - 1)
                sp.dma_start(xT_sb[k % 2], xT[:, k * BLK:(k + 1) * BLK]).then_inc(S[f"xT_in{k % 2}"], 16)
                if k == 1:
                    for dst, src in ((w_out[:, :, :], out_wT), (w_rt[:, :], routerT), (gam, gamma), (bet, beta)):
                        sp.dma_start(dst, src).then_inc(S["params_late"], 16)
            for k in range(NBLK):
                if k < 2:
                    sp.wait_ge(S["a_mm"], NBLK - 1 + k)
                else:
                    sp.wait_ge(S["c_x2"], k - 1)
                sp.dma_start(xT_sb[k % 2], xT[:, k * BLK:(k + 1) * BLK]).then_inc(S[f"cT_in{k % 2}"], 16)
                if k == 0:
                    sp.wait_ge(S["tb_place_act"], 16 - O_POOL)
                    sp.wait_ge(S["tb_place_pool"], O_POOL)
                if k >= 3:
                    sp.wait_ge(S["c_r"], k - 2)
                sp.dma_start(x_in[k % 3], x_tiles[k]).then_inc(S[f"x_in{k % 3}s"], 16)
                if k == 1:
                    sp.wait_ge(S["a_tr"], NH * NBLK)
                    n1 = nat[0].rearrange("p (e h d) -> p e h d", h=FH, d=DM)
                    n2 = nat[1].rearrange("p (e f) -> p e f", f=FF)
                    sp.dma_start(n1[:, 0, :, :], sw1.rearrange("(h p) d -> p h d", p=P)).then_inc(S["w_in1"], 16)
                    for e in range(NE):
                        sp.dma_start(n1[:, 1 + e, :, :], ew1[e].rearrange("(h p) d -> p h d", p=P)).then_inc(S["w_in1"], 16)
                    sp.wait_ge(S["b_y"], W_AT)
                    sp.dma_start(n2[:, 0, :], sw2).then_inc(S["w_in2"], 16)
                    sp.dma_start(n2[:, 1:, :], ew2.rearrange("e d f -> d e f")).then_inc(S["w_in2"], 16)
            def take(k):
                if k % HB == 0:
                    for m in range(YR):
                        sp.wait_ge(S[f"d_sc{m}"], 16 * (ST // YR) * (k // HB + 1))
                if k >= 4:
                    sp.wait_ge(S["e_n"], TB * (k - 3))
                sp.dma_start(yb[k % 4], routed_tiles[k]).then_inc(S[f"e_in{k % 4}"], 16)

            def give(k):
                sp.wait_ge(S["e_n"], TB * (k + 1))
                sp.dma_start(out_tiles[k], ob[k % 3]).then_inc(S[f"e_out{k % 3}"], 16)

            for g in range(SLOT_TILES // LOAD):
                if g * LOAD % ST == 0:
                    sp.wait_ge(S[f"scat{g * LOAD // ST}"], 16 * HT)
                if g >= RING // LOAD:
                    sp.wait_ge(S["d_t"], (g - RING // LOAD + 1) * LOAD)
                    sp.wait_ge(S["d_id"], g - RING // LOAD + 1)
                at = (g * LOAD) % RING
                sp.dma_start(z_rows[:, at:at + LOAD, :], sorted_slots[:, g * LOAD:(g + 1) * LOAD, :])\
                    .then_inc(S[f"d_in{g % 4}"], 16)
                if g == E_GROUP:
                    for k in range(4):
                        take(k)
                if g >= E_GROUP + 2:
                    give(g - E_GROUP - 2)
                    take(g - E_GROUP + 2)
            for k in range(SLOT_TILES // LOAD - E_GROUP - 2, NBLK):
                give(k)
                if k + 4 < NBLK:
                    take(k + 4)
            for r in range(3):
                sp.wait_ge(S[f"e_out{r}"], 16 * ((NBLK + 2 - r) // 3))

        @block.tensor
        def _(pe):
            mm = nc.tensor.matmul
            pe.wait_ge(S["params_in"], 16 * NPAR)
            pe.wait_ge(S["w3_s"], NH)
            pe.wait_ge(S["consts"], 8)
            for h in range(NH):
                last = nc.tensor.transpose(bank[7][:, h * P:(h + 1) * P], w_nat[:, h, :], ident[:, :])
            last.then_inc(S["w3_t"], 1)
            for k in range(NBLK):
                pe.wait_ge(S[f"xT_in{k % 2}"], 16 * (k // 2 + 1))
                if k >= 2:
                    pe.wait_ge(S["a_evac"], NH * (k - 1))
                    pe.wait_ge(S["a_conv"], 4 * (k - 1) - 2)
                for h in range(NH):
                    mm(bank[2 * (k % 2) + h][:, :], w_in[:, h * P:(h + 1) * P], xT_sb[k % 2],
                       start=True, stop=True).then_inc(S["a_x1"], 1)
                if k == 0:
                    pe.wait_ge(S["w3_c"], 1)
                for h in range(NH):
                    last = mm(bank[4 + 2 * (k % 2) + h][:, :], w_tap3[:, h * P:(h + 1) * P], xT_sb[k % 2],
                              start=True, stop=True)
                last.then_inc(S["a_mm"], 1)

            pe.wait_ge(S["tb_place_act"], 16 - O_POOL)
            pe.wait_ge(S["tb_place_dve"], 8)
            pe.wait_ge(S["tb_place_pool"], O_POOL)
            pe.wait_ge(S["a_tr"], NH * NBLK)
            pe.wait_ge(S["a_evac"], NH * NBLK)

            def chunk_states(i, r, peel):
                if not peel:
                    pe.wait_ge(S["b_h"], i - 1)
                for h in range(NH):
                    last = mm(halved(bank[4 + r]), enter[:, h, bass.ds(i, 1), :].rearrange("p a m -> p (a m)"),
                              u_all[:, :, h, i, :],
                              start=(h == 0), stop=(h == NH - 1))
                last.then_inc(S["b_s"], 1)

            def outputs(i, r, peel, then):
                if not peel:
                    pe.wait_ge(S["b_evac"], (i - 1) * 2)
                for h in range(NH):
                    mm(halved(bank[2 * r + h]), toep[:, h, bass.ds(i, 1), :].rearrange("p a m -> p (a m)"),
                       u_all[:, :, h, i, :], start=True, stop=False)
                then()
                pe.wait_ge(S["b_h"], i + 1)
                hv = states[r].rearrange("p (b c) -> p b c", c=CH)
                for h in range(NH):
                    ov = bank[2 * r + h][:, 0:NC].rearrange("p (b c) -> p b c", c=CH)
                    last = mm(ov[:, :, 1:CH], leave[:, h, bass.ds(i, 1), :].rearrange("p a m -> p (a m)"),
                              hv[:, :, 0:CH - 1], start=False, stop=True)
                last.then_inc(S["b_y"], 1)

            chunk_states(0, 0, True)
            outputs(0, 0, True, lambda: chunk_states(1, 1, True))
            outputs(1, 1, True, lambda: chunk_states(2, 0, False))
            for j in range(1, NI // 2 - 1):
                outputs(j * 2, 0, False, lambda: chunk_states(j * 2 + 1, 1, False))
                outputs(j * 2 + 1, 1, False, lambda: chunk_states(j * 2 + 2, 0, False))
            outputs(NI - 2, 0, False, lambda: chunk_states(NI - 1, 1, False))
            outputs(NI - 1, 1, False, lambda: None)

            def x2(k):
                pe.wait_ge(S[f"cT_in{k % 2}"], 16 * (k // 2 + 1))
                if k:
                    pe.wait_ge(S["c_gate"], NH * k)
                else:
                    pe.wait_ge(S["b_evac"], 2 * NI)
                for h in range(NH):
                    last = mm(bank[h][:, :], w_in[:, DI + h * P:DI + (h + 1) * P], xT_sb[k % 2], start=True, stop=True)
                last.then_inc(S["c_x2"], 1)

            def project(k):
                pe.wait_ge(S["c_mul_p"], k + 1)
                pe.wait_ge(S["c_mul_v"], k + 1)
                if k == 0:
                    pe.wait_ge(S["params_late"], 16 * 4)
                if k >= 2:
                    pe.wait_ge(S["c_r"], k - 1)
                for j in range(TB):
                    for h in range(NH):
                        last = mm(bank[2 + k % 2][:, j * P:(j + 1) * P], yT[k % 3][h].rearrange("p (m j) -> p j m", j=TB)[:, j, :],
                                  w_out[:, h, :], start=(h == 0), stop=(h == NH - 1))
                last.then_inc(S["c_out"], 1)

            def turn_z(k):
                pe.wait_ge(S["c_z"], TB * (k + 1))
                if k >= 2:
                    pe.wait_ge(S["c_hT"], k - 1)
                for j in range(TB):
                    last = nc.tensor.transpose(bank[4 + k % 2][:, j * P:(j + 1) * P], z_rows[:, TB * k + j, 0:DM],
                                               ident[:, :])
                last.then_inc(S["c_zt"], 1)

            def route(k):
                pe.wait_ge(S["c_hT"], k + 1)
                for j in range(TB):
                    last = mm(bank[6 + k // HB][:, NE * (TB * (k % HB) + j):NE * (TB * (k % HB) + j + 1)], hT[:, k, j * P:(j + 1) * P], w_rt[:, :],
                              start=True, stop=True)
                last.then_inc(S["c_l"], 1)

            def count(a):
                pe.wait_ge(S["r_dve"], a * R_SLOT + R_HOT)
                mm(bank[6][:, 0:256], tri, rt[a][0].rearrange("p e t -> p (e t)"), start=True, stop=True)
                mm(bank[6][:, 256:512], ones, rt[a][0].rearrange("p e t -> p (e t)"), start=True,
                   stop=True).then_inc(S["r_pe"], 1)

            def up(k):
                if k >= 2:
                    pe.wait_ge(S["s_act"], FH * (k - 1))
                for h in range(FH):
                    last = mm(bank[2 * (k % 2) + h][:, :], w1T[:, h * P:(h + 1) * P], hT[:, k, :], start=True, stop=True)
                last.then_inc(S["s_up"], 1)

            def down(k):
                pe.wait_ge(S["s_act"], FH * (k + 1))
                if k >= 2:
                    pe.wait_ge(S["s_add"], k - 1)
                for j in range(TB):
                    for h in range(FH):
                        last = mm(bank[4 + k % 2][:, j * P:(j + 1) * P], h1[k % 2][h][:, j * P:(j + 1) * P],
                                  w2T[:, h * P:(h + 1) * P], start=(h == 0), stop=(h == FH - 1))
                last.then_inc(S["s_dn"], 1)

            def turn_w(g):
                last_row = tern_block(4 * g + 3)[1]
                pe.wait_ge(S["w_s"], last_row + 1)
                if g:
                    pe.wait_ge(S["w_c"], g)
                for m in range(4):
                    last = nc.tensor.transpose(bank[7][:, m * P:(m + 1) * P], tern_block(4 * g + m)[0], ident[:, :])
                last.then_inc(S["w_t"], 1)

            x2(0)
            x2(1)
            for k in range(NBLK + 4):
                if k < NBLK:
                    project(k)
                if k == R_AT + 2:
                    count(0)
                if k + 2 < NBLK:
                    x2(k + 2)
                if HB - 3 <= k <= HB + 1:
                    turn_w(2 * (k - HB + 3))
                if k == NBLK + 2:
                    pe.wait_ge(S["c_hT"], NBLK - 1)
                    down(0)
                if 3 <= k < NBLK + 3:
                    turn_z(k - 3)
                if k >= 4:
                    route(k - 4)
                if HB - 3 <= k <= HB:
                    turn_w(2 * (k - HB + 3) + 1)
                if k == NBLK:
                    pe.wait_ge(S["c_gate"], NH * NBLK)
                    pe.wait_ge(S["w_c"], 9)
                    up(0)
                if k == NBLK + 1:
                    pe.wait_ge(S["c_r"], NBLK)
                    up(1)

            down(1)
            up(2)
            up(3)
            count(1)
            def turn(j):
                pe.wait_ge(S[f"d_in{j // LOAD % 4}"], 16 * (j // RING + 1))
                if j >= 2:
                    pe.wait_ge(S["d_h"], j - 1)
                nc.tensor.transpose(bank[j % 2][:, 0:P], zt[j % RING][:, 0:DM], ident[:, :]).then_inc(S["d_t"], 1)

            for k in range(2, S_MAIN):
                if 3 <= k < S_MAIN - 1:
                    up(k + 1)
                if k == S_MAIN - 1:
                    pe.wait_ge(S["s_act"], FH * S_MAIN)
                    turn(0)
                    turn(1)
                down(k)

            pe.wait_ge(S["s_act"], FH * S_MAIN)
            pe.wait_ge(S["s_add"], S_MAIN)
            pe.wait_ge(S["r_dve"], R_LAST)

            def expert_up(j):
                pe.wait_ge(S["d_h"], j + 1)
                pe.wait_ge(S["d_w"], j + 1)
                if j >= 2:
                    pe.wait_ge(S["d_act"], j - 1)
                for h in range(FH):
                    last = mm(bank[2 + j % 2][:, h * P:(h + 1) * P], ws[j % 4][:, 0, h * P:(h + 1) * P], hb[j % 4],
                              start=True, stop=True)
                last.then_inc(S["d_up"], 1)

            def expert_down(j):
                pe.wait_ge(S["d_act"], j + 1)
                if j >= 2:
                    pe.wait_ge(S["d_y"], j - 1)
                for h in range(FH):
                    last = mm(bank[4 + j % 2][:, 0:DM], ab[j % 4][:, h * P:(h + 1) * P],
                              ws[j % 4][:, 1, h * P:(h + 1) * P], start=(h == 0), stop=(h == FH - 1))
                last.then_inc(S["d_o"], 1)

            def up_late(k):
                if k > S_MAIN:
                    pe.wait_ge(S["s_add"], k)
                for h in range(FH):
                    last = mm(bank[6 + h][:, :], w1T[:, h * P:(h + 1) * P], hT[:, k, :], start=True, stop=True)
                last.then_inc(S["s_up"], 1)

            def down_late(k):
                pe.wait_ge(S["s_act"], FH * (k + 1))
                for j in range(TB):
                    for h in range(FH):
                        last = mm(bank[6][:, j * P:(j + 1) * P], h1[k % 2][h][:, j * P:(j + 1) * P],
                                  w2T[:, h * P:(h + 1) * P], start=(h == 0), stop=(h == FH - 1))
                last.then_inc(S["s_dn"], 1)

            for j in range(SLOT_TILES + 4):
                if 2 <= j < SLOT_TILES:
                    turn(j)
                if 2 <= j < SLOT_TILES + 2:
                    expert_up(j - 2)
                if j >= 4:
                    expert_down(j - 4)
                if j in S_TILE:
                    up_late(S_MAIN + S_TILE.index(j))
                if j - 3 in S_TILE:
                    down_late(S_MAIN + S_TILE.index(j - 3))

        @block.scalar
        def _(act):
            af = nc.scalar.activation
            for dst, src in ((in_b_sb, in_b), (conv_w_sb, conv_w), (conv_b_sb, conv_b), (w_in[:, :], in_wT)):
                act.dma_start(dst, src).then_inc(S["params_in"], 16)
            act.wait_ge(S["params_in"], 16 * NPAR)
            af(dt_, logdt, ACT.Exp).then_inc(S["tb_act"], 1)
            af(aexp, alog, ACT.Exp).then_inc(S["tb_act"], 1)
            act.wait_ge(S["tb_dve"], 6)
            af(pw, pw, ACT.Exp).then_inc(S["tb_act"], 1)
            def evac(k):
                if k >= 2:
                    act.wait_ge(S["a_conv"], 4 * (k - 1))
                    act.wait_ge(S["a_tmp"], NH * (k - 1))
                for h in range(NH):
                    act.wait_ge(S["a_x1"], NH * k + h + 1)
                    af(x1p[k % 2][h][:, :, TAPS - 1:], bank[2 * (k % 2) + h][:, :].rearrange("p (b t) -> p b t", b=BB),
                       ACT.Identity, bias=in_b_sb[:, h:h + 1]).then_inc(S["a_evac"], 1)

            def first_tap(k, h):
                act.wait_ge(S["a_evac"], NH * k + h + 1)
                if k:
                    act.wait_ge(S["a_add"], NH * (k - 1) + h + 1)
                af(tmp[h].rearrange("p (b t) -> p b t", b=BB), x1p[k % 2][h][:, :, 0:SEQ], ACT.Copy,
                   scale=conv_w_sb[:, h, 0:1]).then_inc(S["a_tmp"], 1)

            act.wait_ge(S["consts"], 8)
            act.wait_ge(S["tb_dve"], 7)
            act.wait_ge(S["w3_t"], 1)
            af(w_tap3, bank[7][:, 0:DI], ACT.Copy).then_inc(S["w3_c"], 1)
            evac(0)
            for h in range(NH):
                first_tap(0, h)
            def place(n):
                h, q = divmod(n % 8, 4)
                rows = slice(32 * q, 32 * q + 32)
                if n < 8:
                    af(toep[rows, h, :, 32 * q:32 * q + 32],
                       ttr[rows, h, :, :].rearrange("p t i -> p i t")[:, :, ::-1],
                       ACT.Copy).then_inc(S["tb_place_act"], 1)
                else:
                    af(leave[rows, h, :, 32 * q:32 * q + 32], otr[rows, h, :, :].rearrange("p t i -> p i t"),
                       ACT.Copy).then_inc(S["tb_place_act"], 1)

            for k in range(NBLK):
                if k + 1 < NBLK:
                    evac(k + 1)
                for h in range(NH):
                    act.wait_ge(S["a_add"], NH * k + h + 1)
                    af(acc[k % 3][h], acc[k % 3][h], ACT.Silu, bias=tap_bias[:, h:h + 1]).then_inc(S["a_silu"], 1)
                if k + 1 < NBLK:
                    for h in range(NH):
                        first_tap(k + 1, h)
                if k == 0:
                    act.wait_ge(S["tb_zero"], 4)
                    act.wait_ge(S["tb_dve"], TB_TR)
                    for n in range(4):
                        place(n)
                elif k <= 2:
                    place(2 + 2 * k)
                    place(3 + 2 * k)
                elif k < 3 + 8 - O_POOL:
                    place(8 + O_POOL + k - 3)

            def b_evac(i, r):
                act.wait_ge(S["b_y"], i + 1)
                for h in range(NH):
                    af(u_all[:, :, h, bass.ds(i, 1), :].rearrange("p a x c -> p a (x c)"), halved(bank[2 * r + h]),
                       ACT.Copy).then_inc(S["b_evac"], 1)

            with act.Fori(0, NI // 2) as j:
                b_evac(j * 2, 0)
                b_evac(j * 2 + 1, 1)

            def gates(k):
                act.wait_ge(S["c_x2"], k + 1)
                if k >= 2:
                    act.wait_ge(S["c_mul_p"], k - 1)
                    act.wait_ge(S["c_mul_v"], k - 1)
                elif k == 0:
                    act.wait_ge(S["b_y"], NI)
                    act.wait_ge(S["fill_in"], 16 * (SLOT_TILES // FILL))
                for h in range(NH):
                    af(gate[k % 2][h], bank[h][:, :], ACT.Silu, bias=in_b_sb[:, 2 + h:3 + h]).then_inc(S["c_gate"], 1)

            def norm_T(k):
                act.wait_ge(S["c_zt"], k + 1)
                if k == 0:
                    act.wait_ge(S["params_late"], 16 * 4)
                if k == NBLK - 4:
                    act.wait_ge(S["r_dve"], R_SLOT)
                af(hT[:, k, :], bank[4 + k % 2][:, :], ACT.Identity, bias=bet, scale=gam).then_inc(S["c_hT"], 1)

            def ffn_norm(k):
                act.wait_ge(S["c_xn"], TB * (k + 1))
                if k == 0:
                    act.wait_ge(S["r_cst"], 9)
                    act.wait_ge(S["w_sub"], 2 * WC)
                for j in range(TB):
                    af(z_rows[:, TB * k + j, 0:DM], xn[:, TB * k + j, :], ACT.Copy,
                       scale=rsd[k % 2][:, 1, j:j + 1]).then_inc(S["c_z"], 1)

            gates(0)
            gates(1)
            def hidden(k):
                act.wait_ge(S["s_up"], k + 1)
                if k == 0:
                    act.wait_ge(S["c_ytr"], NH * NBLK)
                if k >= 2:
                    act.wait_ge(S["s_dn"], k - 1)
                for h in range(FH):
                    af(h1[k % 2][h], bank[2 * (k % 2) + h][:, :], ACT.Silu).then_inc(S["s_act"], 1)

            def scale_rows(k):
                for r in range(6 * k, min(6 * k + 6, WR[0] + WR[1])):
                    n = 0 if r < WR[0] else 1
                    c = (r - n * WR[0]) * WD[n] // 512
                    act.wait_ge(S["w_sub"], WC * n + c + 1)
                    af(tern_row(r), tern_row(r), ACT.Copy, scale=scales[:, r:r + 1]).then_inc(S["w_s"], 1)

            def keep_w(g):
                act.wait_ge(S["w_t"], g + 1)
                if g == 0:
                    act.wait_ge(S["c_ytr"], NH * HB)
                af(u_reg[:, 512 * g:512 * (g + 1)], bank[7][:, :], ACT.Copy).then_inc(S["w_c"], 1)

            for k in range(NBLK + 3):
                if k + 2 < NBLK:
                    gates(k + 2)
                if HB - 3 <= k <= HB + 1:
                    keep_w(2 * (k - HB + 3))
                if 3 <= k:
                    norm_T(k - 3)
                if HB - 3 <= k <= HB:
                    keep_w(2 * (k - HB + 3) + 1)
                if k == NBLK or k == NBLK + 1:
                    hidden(k - NBLK)
                if 1 <= k <= NBLK:
                    ffn_norm(k - 1)
                if k < 5:
                    scale_rows(k)


            for k in range(2, S_MAIN):
                hidden(k)
                if k == EXP_AT:
                    act.wait_ge(S["r_dve"], R_LAST)
                    af(logits[:, :, :], logits[:, :, :], ACT.Exp).then_inc(S["r_exp"], 1)

            def d_norm(j):
                act.wait_ge(S["d_t"], j + 1)
                if j >= 4:
                    act.wait_ge(S["d_up"], j - 3)
                af(hb[j % 4], bank[j % 2][:, 0:P], ACT.Identity, bias=bet, scale=gam).then_inc(S["d_h"], 1)

            def d_silu(j):
                act.wait_ge(S["d_up"], j + 1)
                if j >= 4:
                    act.wait_ge(S["d_o"], j - 3)
                af(ab[j % 4], bank[2 + j % 2][:, 0:FF], ACT.Silu).then_inc(S["d_act"], 1)

            def e_norm(k, j):
                if j == 0:
                    act.wait_ge(S["e_m"], k + 1)
                    if k >= 3:
                        act.wait_ge(S[f"e_out{k % 3}"], 16 * (k // 3))
                af(ob[k % 3][:, j, :], yb[k % 4][:, j, :], ACT.Identity, bias=norm[k % 4][:, 2, j:j + 1],
                   scale=norm[k % 4][:, 1, j:j + 1]).then_inc(S["e_n"], 1)

            for j in range(SLOT_TILES + 2):
                if j < SLOT_TILES:
                    d_norm(j)
                if j >= 2:
                    d_silu(j - 2)
                if j - 1 in S_TILE:
                    k = S_MAIN + S_TILE.index(j - 1)
                    act.wait_ge(S["s_up"], k + 1)
                    act.wait_ge(S["s_dn"], k - 1)
                    for h in range(FH):
                        af(h1[k % 2][h], bank[6 + h][:, :], ACT.Silu).then_inc(S["s_act"], 1)
                if j >= E_AT + E_NORM:
                    e_norm(*divmod(j - E_AT - E_NORM, TB))

            for n in range(SLOT_TILES + 2 - E_AT - E_NORM, NT):
                e_norm(*divmod(n, TB))

        @block.vector
        def _(dve):
            v = nc.vector
            n_tb = [0]

            def table(ins):
                ins.then_inc(S["tb_dve"], 1)
                n_tb[0] += 1

            def settled():
                dve.wait_ge(S["tb_dve"], n_tb[0])

            v.memset(e_reg[:, 0:6144], 0.0).then_inc(S["tb_zero_dve"], 1)
            dve.wait_ge(S["params_in"], 16 * NPAR)
            for h in range(NH):
                v.tensor_scalar(w_nat[:, h, :], w_nat[:, h, :], conv_w_sb[:, h, TAPS - 1:TAPS], None,
                                ALU.mult).then_inc(S["w3_s"], 1)
            table(v.tensor_tensor(tap_bias, in_b_sb[:, 0:NH], conv_w_sb[:, :, TAPS - 1], ALU.mult))
            dve.wait_ge(S["tb_act"], 2)
            dtb = dt_.rearrange("p (h a) -> p h a", a=1).broadcast_to([P, NH, NST])
            table(v.tensor_tensor(a_, aexp, dtb, ALU.mult))
            table(v.tensor_tensor(db, bpar, dtb, ALU.mult))
            settled()
            table(v.tensor_tensor(wk, db, cpar, ALU.mult))
            dve.wait_ge(S["consts"], 8)

            def wide(ap):
                return ap.rearrange("p h n -> p (h n)").rearrange("p (m a) -> p m a", a=1).broadcast_to([P, NH * NST, L])

            def times(ap):
                return ap.rearrange("p (a t) -> p a t", a=1).broadcast_to([P, NH * NST, L])

            def flat(ap):
                return ap.rearrange("p h n t -> p (h n) t")

            table(v.tensor_tensor(flat(pw_r), wide(a_), times(t_rev), ALU.mult))
            table(v.tensor_tensor(flat(pw_f), wide(a_), times(t_fwd), ALU.mult))
            v.memset(e_reg[:, 6144:], 0.0).then_inc(S["tb_zero_dve"], 1)
            dve.wait_ge(S["tb_act"], 3)
            table(v.tensor_tensor(tap_bias, tap_bias, conv_b_sb, ALU.add))
            table(v.tensor_tensor(flat(esrc), flat(pw_r), wide(db), ALU.mult))
            table(v.tensor_tensor(flat(ksrc), flat(pw_r), wide(wk), ALU.mult))
            dve.wait_ge(S["tb_zero"], 2)
            for h in range(NH):
                table(v.tensor_tensor(osrc[:, h, :, 16 * h:16 * h + 16], pw_f[:, h, :, :].rearrange("p n t -> p t n"),
                                      cpar[:, h, :].rearrange("p (a n) -> p a n", a=1).broadcast_to([P, L, NST]), ALU.mult))
            table(v.tensor_copy(dsrc.rearrange("p (h n) -> p h n", h=NH), pw_f[:, :, :, L - 1]))
            def conv(k):
                dve.wait_ge(S["a_mm"], k + 1)
                if k >= 3:
                    dve.wait_ge(S["a_tr"], NH * (k - 2))
                for n, tap in enumerate((2, 1)):
                    for h in range(NH):
                        if n == 0:
                            dve.wait_ge(S["a_evac"], NH * k + h + 1)
                        else:
                            dve.wait_ge(S["a_conv"], 4 * k + h + 1)
                        av = acc[k % 3][h].rearrange("p (b t) -> p b t", b=BB)
                        prev = bank[4 + 2 * (k % 2) + h][:, :].rearrange("p (b t) -> p b t", b=BB) if n == 0 else av
                        v.scalar_tensor_tensor(out=av, in0=x1p[k % 2][h][:, :, tap:tap + SEQ],
                                               scalar=conv_w_sb[:, h, tap:tap + 1], in1=prev, op0=ALU.mult,
                                               op1=ALU.add).then_inc(S["a_conv"], 1)

            conv(0)
            settled()
            for h in range(NH):
                table(v.tensor_reduce(kpad[:, h, 0:L], ksrc[:, h, :, :].rearrange("p n t -> p t n"), AX.X, ALU.add))
                table(v.transpose(etr[:, h, :, :].rearrange("p n i -> p (n i)"), esrc[:, h, :, :].rearrange("p n t -> p (n t)")))
                table(v.transpose(otr[:, h, :, :].rearrange("p t i -> p (t i)"), osrc[:, h, :, :].rearrange("p t s -> p (t s)")))
            table(v.transpose(decay[:, :], dsrc))
            settled()
            for h in range(NH):
                table(v.transpose(ttr[:, h, :, :], windows[h]))
            assert n_tb[0] == TB_TR, n_tb[0]
            settled()

            def place_enter():
                dve.wait_ge(S["tb_zero_dve"], 2)
                for h in range(NH):
                    for q in range(4):
                        rows = slice(32 * q, 32 * q + 32)
                        v.tensor_copy(enter[rows, h, :, 32 * q + 16 * h:32 * q + 16 * h + 16],
                                      etr[rows, h, :, :].rearrange("p n i -> p i n")).then_inc(S["tb_place_dve"], 1)

            def spread(k):
                dve.wait_ge(S["a_silu"], NH * (k + 1))
                if k == HB:
                    dve.wait_ge(S["tb_place_dve"], 8)
                    dve.wait_ge(S["tb_place_act"], 8)
                for h in range(NH):
                    v.transpose(u_all[:, k // HB, h, :, CB * (k % HB):CB * (k % HB + 1)].rearrange("p i c -> p c i"),
                                acc[k % 3][h].rearrange("p (c t) -> p c t", t=L)).then_inc(S["a_tr"], 1)

            for k in range(NBLK):
                if k + 1 < NBLK:
                    conv(k + 1)
                spread(k)
                if k == 0:
                    place_enter()

            def scan(i, r, peel):
                dve.wait_ge(S["b_s"], i + 1)
                dve.wait_ge(S["b_d0"], i + 1)
                if not peel:
                    dve.wait_ge(S["b_y"], i - 1)
                v.tensor_tensor_scan(states[r], decay_row[r], bank[4 + r][:, 0:NC], 0.0, ALU.mult,
                                     ALU.add).then_inc(S["b_h"], 1)

            scan(0, 0, True)
            scan(1, 1, True)
            n_w = [0]

            def w_step(make):
                if n_w[0]:
                    dve.wait_ge(S["w_q"], n_w[0])
                make().then_inc(S["w_q"], 1)
                n_w[0] += 1

            def w_scale(n, c):
                cols, rows = chunk(n, c)
                if c == 0:
                    dve.wait_ge(S[f"w_in{n + 1}"], 16 * (NE + 1 if n == 0 else 2))
                w_step(lambda: v.tensor_reduce(scale[n][:, rows], nat[n][:, cols].rearrange("p (r d) -> p r d", d=WD[n]),
                                               AX.X, ALU.add, apply_absolute_value=True))
                if c == WC - 1:
                    w_step(lambda: v.tensor_scalar(scale[n], scale[n], 1.0 / WD[n], EPS, ALU.mult, ALU.max))
                    w_step(lambda: v.tensor_scalar(above[n], scale[n], 0.5, None, ALU.mult))
                    w_step(lambda: v.tensor_scalar(below[n], scale[n], -0.5, None, ALU.mult))

            def w_compare(n, c, low):
                cols, rows = chunk(n, c)
                bound = (below if low else above)[n][:, rows].rearrange("p (r a) -> p r a", a=1)\
                    .broadcast_to([P, rows.stop - rows.start, WD[n]])
                w = nat[n][:, cols].rearrange("p (r d) -> p r d", d=WD[n])
                to = w if low else tern[n][:, cols].rearrange("p (r d) -> p r d", d=WD[n])
                if not low and n == 0 and c == 0:
                    dve.wait_ge(S["b_y"], W_AT)
                w_step(lambda: v.tensor_tensor(to, w, bound, ALU.is_lt if low else ALU.is_gt))
                if low:
                    assert n_w[0] == W_LOW[n] + c + 1, n_w[0]

            with dve.Fori(1, 6) as j:
                scan(j * 2, 0, False)
                scan(j * 2 + 1, 1, False)
            for i in range(12, NI):
                scan(i, i % 2, False)
                if W_AT - WC <= i < W_AT:
                    w_scale(0, i - W_AT + WC)
                if i >= W_AT:
                    for n in range(2 * (i - W_AT), 2 * (i - W_AT) + 2):
                        stage, c = divmod(n, WC)
                        if stage == 0 or stage == 1:
                            w_compare(0, c, stage == 1)
                        elif stage == 2:
                            w_scale(1, c)
                        elif stage == 3 or stage == 4:
                            w_compare(1, c, stage == 4)

            def gather(k, h):
                v.transpose(yT[k % 3][h].rearrange("p (c t) -> p c t", t=L),
                            u_all[:, k // HB, h, :, CB * (k % HB):CB * (k % HB + 1)].rearrange("p i c -> p c i"))\
                    .then_inc(S["c_ytr"], 1)

            def gate_mul(k):
                dve.wait_ge(S["c_gate"], NH * (k + 1))
                dve.wait_ge(S["c_ytr"], NH * (k + 1))
                v.tensor_tensor(yT[k % 3][1], yT[k % 3][1], gate[k % 2][1], ALU.mult).then_inc(S["c_mul_v"], 1)

            def residual(k):
                dve.wait_ge(S["c_out"], k + 1)
                dve.wait_ge(S["c_xb"], k + 1)
                if k >= 2:
                    dve.wait_ge(S["c_xn"], TB * (k - 1))
                v.tensor_tensor(res[k % 2], bank[2 + k % 2][:, :].rearrange("p (j d) -> p j d", j=TB),
                                x_in[k % 3], ALU.add).then_inc(S["c_r"], 1)

            def bn_sums(k):
                dve.wait_ge(S["c_r"], k + 1)
                for j in range(TB):
                    v.bn_stats(stats[k % 2][:, j, :], res[k % 2][:, j, :]).then_inc(S["c_st"], 1)

            def bn_join(k):
                if k >= 2:
                    dve.wait_ge(S["c_rs"], k - 1)
                for j in range(TB):
                    dve.wait_ge(S["c_st"], TB * k + j + 1)
                    v.bn_aggr(mv[k % 2][:, j, :], stats[k % 2][:, j, :]).then_inc(S["c_ag"], 1)

            def variances(k, between):
                t, var = rs[k % 2], mv[k % 2][:, :, 1]
                dve.wait_ge(S["c_ag"], TB * (k + 1))
                v.tensor_scalar(t[:, 0, :], var, EPS, None, ALU.add).then_inc(S["c_u"], 1)
                between(0)
                dve.wait_ge(S["c_u"], 4 * k + 1)
                v.reciprocal(t[:, 2, :], t[:, 0, :]).then_inc(S["c_u"], 1)
                between(1)
                dve.wait_ge(S["c_u"], 4 * k + 2)
                v.tensor_tensor(t[:, 3, :], t[:, 2, :], var, ALU.mult).then_inc(S["c_u"], 1)
                dve.wait_ge(S["c_u"], 4 * k + 3)
                v.tensor_scalar(t[:, 1, :], t[:, 3, :], EPS, None, ALU.add).then_inc(S["c_u"], 1)

            def normalise(k):
                dve.wait_ge(S["c_rs"], k + 1)
                if k == HB:
                    dve.wait_ge(S["w_t"], WC)
                for j in range(TB):
                    v.tensor_scalar(xn[:, TB * k + j, :], res[k % 2][:, j, :], mv[k % 2][:, j, 0:1],
                                    rsd[k % 2][:, 0, j:j + 1], ALU.subtract, ALU.mult).then_inc(S["c_xn"], 1)

            n_r = [0]

            def r_step(ins):
                ins.then_inc(S["r_dve"], 1)
                n_r[0] += 1
                dve.wait_ge(S["r_dve"], n_r[0])

            def over_t(ap):
                return ap.rearrange("p (e a) -> p e a", a=1).broadcast_to([P, NE, HT])

            def over_e(ap, n=HT):
                return ap.rearrange("p (a t) -> p a t", a=1).broadcast_to([P, NE, n])

            def by_t(ap):
                return ap.rearrange("p e t -> p t e")

            def part(a, at, width):
                return route_scratch[a][:, 1024 + at:1024 + at + width]

            def pick(a):
                mx, best = top_p[:, HT * a:HT * (a + 1)], part(a, 0, HT)
                hot = rt[a][0]
                lg = logits[:, :, HT * a:HT * (a + 1)]
                dve.wait_ge(S["c_l"], HB * (a + 1))
                dve.wait_ge(S["r_cst"], 9)
                r_step(v.tensor_copy(lg.rearrange("p e t -> p t e"), bank[6 + a][:, 0:256]
                                     .rearrange("p (t e) -> p t e", e=NE)))
                r_step(v.tensor_reduce(mx, by_t(lg), AX.X, ALU.max))
                r_step(v.tensor_tensor(hot, lg, over_e(mx), ALU.is_equal))
                r_step(v.tensor_tensor(hot, hot, wide8[:, :, :], ALU.mult))
                r_step(v.tensor_reduce(best, by_t(hot), AX.X, ALU.max))
                r_step(v.tensor_tensor(hot, wide8[:, :, :], over_e(best), ALU.is_equal))
                assert n_r[0] == a * R_SLOT + R_HOT

            def place(a):
                hot, run, rank = rt[a][0:3]
                posf = part(a, 2 * HT, HT)
                cnt_i, tiles, base = part(a, 136, NE).bitcast(I32), part(a, 144, NE), part(a, 160, NE)
                tot = bank[6][:, 256:512]
                dve.wait_ge(S["r_pe"], a + 1)
                r_step(v.tensor_tensor_scan(run.rearrange("p e t -> p (e t)"), lead_mask.rearrange("p e t -> p (e t)"),
                                            tot, 0.0, ALU.mult, ALU.add))
                r_step(v.tensor_scalar(cnt_i, run[:, :, HT - 1], float(P - 1), None, ALU.add))
                r_step(v.tensor_tensor(rank, bank[6][:, 0:256].rearrange("p (e t) -> p e t", e=NE), run, ALU.add))
                r_step(v.tensor_scalar(cnt_i, cnt_i, 7, None, ALU.arith_shift_right))
                r_step(v.tensor_copy(tiles, cnt_i))
                r_step(v.tensor_tensor_scan(upto[a][:, :], one8, tiles, 0.0, ALU.mult, ALU.add))
                r_step(v.tensor_tensor(base, upto[a][:, :], tiles, ALU.subtract))
                r_step(v.scalar_tensor_tensor(out=rank, in0=over_t(base), scalar=float(P), in1=rank, op0=ALU.mult,
                                              op1=ALU.add))
                r_step(v.tensor_tensor(rank, rank, hot, ALU.mult))
                r_step(v.tensor_reduce(posf, by_t(rank), AX.X, ALU.add))
                r_step(v.tensor_scalar(slot[:, HT * a:HT * (a + 1)], posf, float(a * P * ST), None, ALU.add))
                assert n_r[0] == (a + 1) * R_SLOT, n_r[0]

            def tile_experts(a):
                ej = work[:, 0:ST * NE].rearrange("p (j e) -> p j e", e=NE)
                ef = work[:, 512:512 + ST]
                r_step(v.tensor_tensor(ej, tile_no[:, :].rearrange("p (j a) -> p j a", a=1).broadcast_to([P, ST, NE]),
                                       upto[a][:, :].rearrange("p (a e) -> p a e", a=1).broadcast_to([P, ST, NE]), ALU.is_ge))
                r_step(v.tensor_reduce(ef, ej, AX.X, ALU.add))
                r_step(v.tensor_scalar(weights_at[:, ST * a:ST * (a + 1)], ef, float(NE - 1), float(FF), ALU.min, ALU.mult))

            dve.wait_ge(S["b_evac"], 2 * NI)
            dve.wait_ge(S["fill_in"], 16 * (SLOT_TILES // FILL))
            dve.wait_ge(S["w_sub"], WC)
            for k in range(3):
                for h in range(NH):
                    gather(k, h)
            gate_mul(0)
            for k in range(NBLK + 1):
                if k < NBLK:
                    residual(k)
                if k + 1 < NBLK:
                    gate_mul(k + 1)
                if k < NBLK:
                    bn_sums(k)
                if 1 <= k <= NBLK:
                    normalise(k - 1)
                if k < NBLK:
                    bn_join(k)
                if k < NBLK:
                    variances(k, lambda h: gather(k + 3, h) if k + 3 < NBLK else None)
                if k == R_AT:
                    pick(0)
                if k == R_AT + 1:
                    place(0)
            dve.wait_ge(S["c_out"], NBLK)
            def add_shared(k, src):
                dve.wait_ge(S["s_dn"], k + 1)
                xv = xn[:, TB * k:TB * (k + 1), :]
                v.tensor_tensor(xv, src[:, :].rearrange("p (j d) -> p j d", j=TB), xv, ALU.add).then_inc(S["s_add"], 1)

            add_shared(0, bank[4])
            pick(1)
            add_shared(1, bank[5])
            place(1)
            add_shared(2, bank[4])
            r_step(v.tensor_tensor(logits[:, :, :], logits[:, :, :], over_e(top_p[:, :], NT), ALU.subtract))
            tile_experts(0)
            add_shared(3, bank[5])
            tile_experts(1)
            assert n_r[0] == R_LAST

            for k in range(4, S_MAIN):
                add_shared(k, bank[4 + k % 2])
                if k == EXP_AT + 1:
                    dve.wait_ge(S["r_exp"], 1)
                    v.tensor_reduce(top_p[:, :], by_t(logits[:, :, :]), AX.X, ALU.add).then_inc(S["p_sum"], 1)
                    dve.wait_ge(S["p_sum"], 1)
                    v.reciprocal(top_p[:, :], top_p[:, :]).then_inc(S["p_sum"], 1)
                    dve.wait_ge(S["p_sum"], 2)

            at_regs = [dve.alloc_register(f"weights_at{n}") for n in range(LOAD)]

            def fetch(j):
                if j % LOAD == 0:
                    dve.load(at_regs, weights_at[0:1, j:j + LOAD])
                at = dve.snap(at_regs[j % LOAD], min_val=0, max_val=(NE - 1) * FF)
                if j >= 4:
                    dve.wait_ge(S["d_o"], j - 3)
                routed = u_reg[:, FF:FF + 2 * GW].rearrange("p (m x) -> p m x", m=2)
                v.tensor_copy(ws[j % 4], routed[:, :, bass.ds(at, FF)]).then_inc(S["d_w"], 1)
                if j % LOAD == 0:
                    g = j // LOAD
                    dve.wait_ge(S[f"d_in{g % 4}"], 16 * (j // RING + 1))
                    if j >= RING:
                        for m in range(LOAD):
                            dve.wait_ge(S[f"d_sc{(j + m) % YR}"], 16 * ((j + m - RING) // YR + 1))
                    at = j % RING
                    v.tensor_copy(ids[:, at:at + LOAD], z_rows[:, at:at + LOAD, DM:ROW].bitcast(I32)
                                  .rearrange("p t a -> p (t a)")).then_inc(S["d_id"], 1)

            def d_rows(j):
                dve.wait_ge(S["d_o"], j + 1)
                if j >= YR:
                    dve.wait_ge(S[f"d_sc{j % YR}"], 16 * (j // YR))
                v.tensor_copy(yt[j % YR], bank[4 + j % 2][:, 0:DM]).then_inc(S["d_y"], 1)

            def e_add(k, j):
                if j == 0:
                    dve.wait_ge(S[f"e_in{k % 4}"], 16 * (k // 4 + 1))
                v.scalar_tensor_tensor(out=yb[k % 4][:, j, :], in0=yb[k % 4][:, j, :],
                                       scalar=top_p[:, TB * k + j:TB * k + j + 1], in1=xn[:, TB * k + j, :],
                                       op0=ALU.mult, op1=ALU.add).then_inc(S["e_y"], 1)

            def e_stats(k, j):
                if k >= HB and j == TB - 1:
                    dve.wait_ge(S["e_py"], k - HB + 1)
                else:
                    dve.wait_ge(S["e_y"], TB * k - max(k - HB, 0) + j + 1)
                v.bn_stats(stats[k % 2][:, j, :], yb[k % 4][:, j, :]).then_inc(S["e_st"], 1)

            def e_join(k, j):
                if j == 0 and k >= 2:
                    dve.wait_ge(S["e_m"], k - 1)
                dve.wait_ge(S["e_st"], TB * k + j + 1)
                v.bn_aggr(mv[k % 2][:, j, :], stats[k % 2][:, j, :]).then_inc(S["e_ag"], 1)
                if j == TB - 1:
                    if k >= 4:
                        dve.wait_ge(S["e_n"], TB * (k - 3))
                    dve.wait_ge(S["e_ag"], TB * (k + 1))
                    v.tensor_scalar(norm[k % 4][:, 0, :], mv[k % 2][:, :, 1], EPS, None, ALU.add).then_inc(S["e_u"], 1)

            def e_shift(k):
                dve.wait_ge(S["e_rs"], k + 1)
                v.scalar_tensor_tensor(out=norm[k % 4][:, 2, :], in0=mv[k % 2][:, :, 0], scalar=-1.0,
                                       in1=norm[k % 4][:, 1, :], op0=ALU.mult, op1=ALU.mult).then_inc(S["e_m"], 1)

            for j in range(SLOT_TILES + 4):
                e_on = j >= E_AT
                if e_on:
                    k, m = divmod(j - E_AT, TB)
                    e_add(k, m)
                if j < SLOT_TILES:
                    fetch(j)
                if e_on:
                    e_stats(k, m)
                if j >= 4:
                    d_rows(j - 4)
                if j - 4 in S_TILE:
                    add_shared(S_MAIN + S_TILE.index(j - 4), bank[6])
                if e_on:
                    e_join(k, m)
                    if m == TB - 1 and k >= 1:
                        e_shift(k - 1)
            for k in range(HB, NBLK):
                for m in range(TB - 1):
                    e_add(k, m)
                for m in range(TB):
                    e_stats(k, m)
                e_shift(k - 1)
                for m in range(TB):
                    e_join(k, m)
            e_shift(NBLK - 1)

        @block.gpsimd
        def _(pool):
            g = nc.gpsimd
            g.dma_start(outb[:, :], out_b.rearrange("(a d) -> a d", a=1).broadcast_to([P, DM])).then_inc(S["outb_in"], 16)
            g.memset(work[:, 1024:3096], 0.0).then_inc(S["consts"], 1)
            g.iota(t_rev, pattern=[[-1, L]], base=L - 1, channel_multiplier=0,
                   allow_small_or_imprecise_dtypes=True).then_inc(S["consts"], 1)
            g.iota(t_fwd, pattern=[[1, L]], base=1, channel_multiplier=0,
                   allow_small_or_imprecise_dtypes=True).then_inc(S["consts"], 1)
            g.memset(ident[:, :], 0.0).then_inc(S["consts"], 1)
            g.memset(first_mask[:, :, :], 1.0).then_inc(S["consts"], 1)
            g.memset(half_neg[:, :], -0.5).then_inc(S["consts"], 1)
            pool.wait_ge(S["consts"], 6)
            g.memset(first_mask[:, :, 0:1], 0.0).then_inc(S["consts"], 1)
            g.affine_select(out=ident[:, :], in_=ident[:, :], compare_op=ALU.not_equal, fill=1.0, base=0,
                            pattern=[[-1, P]], channel_multiplier=1).then_inc(S["consts"], 1)
            for ap in (kpad, osrc, toep, leave):
                g.memset(ap, 0.0).then_inc(S["tb_zero"], 1)
            def place(n):
                h, q = divmod(n, 4)
                rows = slice(32 * q, 32 * q + 32)
                g.tensor_copy(leave[rows, h, :, 32 * q:32 * q + 32],
                              otr[rows, h, :, :].rearrange("p t i -> p i t")).then_inc(S["tb_place_pool"], 1)
                pool.wait_ge(S["tb_place_pool"], n + 1)

            for k in range(NBLK):
                for h in range(NH):
                    pool.wait_ge(S["a_tmp"], NH * k + h + 1)
                    pool.wait_ge(S["a_conv"], 4 * k + 2 + h + 1)
                    g.tensor_tensor(acc[k % 3][h], acc[k % 3][h], tmp[h], ALU.add).then_inc(S["a_add"], 1)
                if k % 3 == 1 and k // 3 < O_POOL:
                    pool.wait_ge(S["tb_zero"], 4)
                    pool.wait_ge(S["tb_dve"], TB_TR)
                    pool.wait_ge(S["a_add"], NH * (k + 1))
                    place(k // 3)

            def multipliers(i, r, peel):
                if not peel:
                    pool.wait_ge(S["b_h"], i - 1)
                g.tensor_tensor(decay_row[r], first_mask[:, :, :].rearrange("p b c -> p (b c)"),
                                decay[:, bass.ds(i, 1)].broadcast_to([P, NC]), ALU.mult).then_inc(S["b_d0"], 1)

            pool.wait_ge(S["a_tr"], NH * NBLK)
            pool.wait_ge(S["consts"], 8)
            multipliers(0, 0, True)
            multipliers(1, 1, True)
            sorted_fill = sorted_rows.rearrange("(n p j) w -> n p j w", j=FILL, p=P)
            for n in range(SLOT_TILES // FILL):
                with pool.Fori(1 + 3 * n, 4 + 3 * n) as j:
                    multipliers(j * 2, 0, False)
                    multipliers(j * 2 + 1, 1, False)
                if n == 0:
                    g.memset(work[:, 2048:2048 + FILL * ROW], 0.0).then_inc(S["unused"], 1)
                pool.wait_ge(S["unused"], n + 1)
                if n:
                    pool.wait_ge(S["fill_in"], 16 * n)
                g.iota(fill[:, :, DM:ROW].bitcast(I32).rearrange("p j a -> p (j a)"), pattern=[[1, FILL]],
                       base=TOK + n * P * FILL, channel_multiplier=FILL).then_inc(S["unused"], 1)
                pool.wait_ge(S["unused"], n + 2)
                g.dma_start(sorted_fill[n], fill).then_inc(S["fill_in"], 16)
                if n == 1:
                    g.memset(lead_mask, 1.0).then_inc(S["r_cst"], 1)
                    g.memset(tri, 0.0).then_inc(S["r_cst"], 1)
                    g.memset(ones, 1.0).then_inc(S["r_cst"], 1)
                    g.memset(one8, 1.0).then_inc(S["r_cst"], 1)
                    g.iota(wide8[:, :, :], pattern=[[-1, NE], [0, HT]], base=NE, channel_multiplier=0,
                           allow_small_or_imprecise_dtypes=True).then_inc(S["r_cst"], 1)
                    g.iota(tile_no[:, :], pattern=[[1, ST]], base=0, channel_multiplier=0,
                           allow_small_or_imprecise_dtypes=True).then_inc(S["r_cst"], 1)
                    pool.wait_ge(S["r_cst"], 6)
                    g.memset(lead_mask[:, :, 0:1], 0.0).then_inc(S["r_cst"], 1)
                    g.affine_select(out=tri, in_=tri, compare_op=ALU.is_gt, fill=-1.0, base=0,
                                    pattern=[[1, P]], channel_multiplier=-1).then_inc(S["r_cst"], 1)
            def w_subtract(m):
                n, c = divmod(m, WC)
                cols, rows = chunk(n, c)
                pool.wait_ge(S["w_q"], W_LOW[n] + c + 1)
                g.tensor_tensor(tern[n][:, cols], tern[n][:, cols], nat[n][:, cols], ALU.subtract)\
                    .then_inc(S["w_sub"], 1)

            for i in range(26, NI):
                multipliers(i, i % 2, False)
                w_subtract(i - 26)
            for m in range(NI - 26, 2 * WC):
                w_subtract(m)
            pool.wait_ge(S["fill_in"], 16 * (SLOT_TILES // FILL))

            def multiply(k):
                pool.wait_ge(S["c_gate"], NH * (k + 1))
                pool.wait_ge(S["c_ytr"], NH * (k + 1))
                g.tensor_tensor(yT[k % 3][0], yT[k % 3][0], gate[k % 2][0], ALU.mult).then_inc(S["c_mul_p"], 1)
                pool.wait_ge(S[f"x_in{k % 3}s"], 16 * (k // 3 + 1))
                g.tensor_tensor(x_in[k % 3], x_in[k % 3],
                                outb[:, :].rearrange("p (a d) -> p a d", a=1).broadcast_to([P, TB, DM]),
                                ALU.add).then_inc(S["c_xb"], 1)

            def rstd(k):
                pool.wait_ge(S["c_u"], 4 * (k + 1))
                if k >= 2:
                    pool.wait_ge(S["c_z"], TB * (k - 1))
                g.tensor_tensor(rsd[k % 2][:, 0:2, :].rearrange("p a j -> p (a j)"), rs[k % 2][:, 0:2, :].rearrange("p a j -> p (a j)"),
                                half_neg[:, :], ALU.pow).then_inc(S["c_rs"], 1)

            pool.wait_ge(S["outb_in"], 16)
            multiply(0)
            multiply(1)
            pool.wait_ge(S["w_sub"], 2 * WC)
            g.iota(z_rows[:, :, DM:ROW].bitcast(I32).rearrange("p t a -> p (t a)"), pattern=[[BLK, NBLK], [1, TB]], base=0,
                   channel_multiplier=TB).then_inc(S["r_cst"], 1)
            def sort_rows(a, first, last):
                if first == 0:
                    pool.wait_ge(S["r_dve"], (a + 1) * R_SLOT)
                for t in range(HT * a + first, HT * a + last):
                    g.indirect_dma_start(sorted_rows, bass.IndirectOffsetOnAxis(ap=slot[:, t:t + 1], axis=0),
                                         z_rows[:, t, :], None).then_inc(S[f"scat{a}"], 16)

            done = 0
            for k in range(NBLK):
                if k + 2 < NBLK:
                    multiply(k + 2)
                rstd(k)
                if R_AT + 1 <= k < NBLK - 1:
                    sort_rows(0, done, done + SORTS)
                    done += SORTS
            sort_rows(0, done, HT)
            sort_rows(1, 0, HT)

            def scatter(j):
                pool.wait_ge(S["d_y"], j + 1)
                pool.wait_ge(S["d_id"], j // LOAD + 1)
                g.indirect_dma_start(routed_out, bass.IndirectOffsetOnAxis(ap=ids[:, j % RING:j % RING + 1], axis=0),
                                     yt[j % YR], None).then_inc(S[f"d_sc{j % YR}"], 16)

            def e_rstd(k):
                pool.wait_ge(S["e_u"], k + 1)
                g.tensor_tensor(norm[k % 4][:, 1, :], norm[k % 4][:, 0, :], half_neg[:, 0:TB],
                                ALU.pow).then_inc(S["e_rs"], 1)

            for j in range(SLOT_TILES):
                scatter(j)
                if E_AT <= j < SLOT_TILES - TB and (j - E_AT) % TB == 0:
                    e_rstd((j - E_AT) // TB)

            def e_add_last(k):
                pool.wait_ge(S[f"e_in{k % 4}"], 16 * (k // 4 + 1))
                row, t = yb[k % 4][:, TB - 1, :], TB * (k + 1) - 1
                g.tensor_tensor(row, row, top_p[:, t:t + 1].broadcast_to([P, DM]), ALU.mult).then_inc(S["e_pm"], 1)
                pool.wait_ge(S["e_pm"], k - HB + 1)
                g.tensor_tensor(row, row, xn[:, t, :], ALU.add).then_inc(S["e_py"], 1)

            for k in range((SLOT_TILES - TB - E_AT) // TB, HB):
                e_rstd(k)
            e_add_last(HB)
            for k in range(HB, NBLK):
                if k + 1 < NBLK:
                    e_add_last(k + 1)
                e_rstd(k)


TB_TR = 21
O_POOL = 2
R_HOT, R_SLOT, R_LAST = 6, 17, 41
R_AT = 11
SORTS = 3
W_AT = 18
W_LOW = (8 + 5, 8 + 5 + 5 + 8 + 5)
EXP_AT = 5
E_AT = 52
S_TILE = (44, 60)
S_MAIN = NBLK - len(S_TILE)
E_NORM = 9
E_GROUP = 15


def kernel(**inputs):
    import numpy as np
    import concourse.bacc as bacc
    from concourse.bass_utils import run_bass_kernel_spmd as run

    a = {k: np.asarray(v) for k, v in inputs.items()}
    rows = np.ascontiguousarray(a["L0_attn_x"].reshape(TOK, DM))

    def halves(w):
        return np.ascontiguousarray(np.moveaxis(w.reshape((-1, P) + w.shape[1:]), 0, 1))

    arrays = {
        "xT": np.ascontiguousarray(rows.T), "x": rows,
        "in_wT": np.ascontiguousarray(a["L0_attn_in_proj_w"].T), "in_w_nat": halves(a["L0_attn_in_proj_w"][:DI]), "in_b": halves(a["L0_attn_in_proj_b"]),
        "conv_w": halves(a["L0_attn_conv_w"].reshape(DI, TAPS)), "conv_b": halves(a["L0_attn_conv_b"]),
        "a_log": halves(a["L0_attn_A_log"]), "b_par": halves(a["L0_attn_B_param"]),
        "c_par": halves(a["L0_attn_C_param"]), "log_dt": halves(a["L0_attn_log_dt"]),
        "out_wT": halves(a["L0_attn_out_proj_w"].T), "out_b": a["L0_attn_out_proj_b"],
        "sw1": a["L0_ffn_shared_w1"], "sw2": a["L0_ffn_shared_w2"], "ew1": a["L0_ffn_expert_w1"],
        "ew2": a["L0_ffn_expert_w2"], "routerT": np.ascontiguousarray(a["L0_ffn_router_w"].T),
        "gamma": a["L0_ffn_ln_gamma"].reshape(DM, 1), "beta": a["L0_ffn_ln_beta"].reshape(DM, 1),
    }
    nc = bacc.Bacc("TRN2", target_bir_lowering=False, num_devices=1)
    args = [nc.dram_tensor(n, v.shape, F32, kind="ExternalInput").ap() for n, v in arrays.items()]
    out = nc.dram_tensor("out", (TOK, DM), F32, kind="ExternalOutput").ap()
    build(nc, *args, out)
    r = run(nc, [arrays], core_ids=[0])
    return r.results[0]["out"].reshape(BATCH, SEQ, DM)
```
